# Optimizing a Trainium2 kernel written in Bass

```python
import numpy as np
import jax
import jax.numpy as jnp

def _softmax(x, axis=-1):
    return jax.nn.softmax(x, axis=axis)

def _gelu(x):
    return jax.nn.gelu(x, approximate=True)

def _silu(x):
    return jax.nn.silu(x)

def _sigmoid(x):
    return jax.nn.sigmoid(x)

def _layernorm(x, axis=-1, eps=1e-05):
    m = jnp.mean(x, axis=axis, keepdims=True)
    v = jnp.var(x, axis=axis, keepdims=True)
    return (x - m) / jnp.sqrt(v + eps)

def _scatter_add(tgt, idx, src, axis=0):
    return tgt.at[idx].add(src)

def _segment_sum(src, seg, n):
    return jax.ops.segment_sum(src, seg, n)
kernel_name = 'mk_gnn_ffn_d1_gnn_r64_30b0cf'

def setup_inputs(seed: int=0):
    np.random.seed(seed)
    _w = jnp.asarray

    def _rec_inputs():
        import jax
        import jax.numpy as jnp
        _gk = jax.random.key(seed)
        x = -6.415e-05 + 1 * jax.random.normal(jax.random.fold_in(_gk, 1), (20000, 512), jnp.float32)
        src = jax.random.randint(jax.random.fold_in(_gk, 2), (10000,), 0, 20000, jnp.int32)
        dst = jnp.minimum((20000 * jax.random.uniform(jax.random.fold_in(_gk, 3), (10000,)) ** 2.0).astype(jnp.int32), 19999)
        _o = jnp.argsort(dst, stable=True)
        src = src[_o]
        dst = dst[_o]
        return (x, src, dst)
    x, src, dst = _rec_inputs()

    def _L0_gnn_setup():
        import jax, jax.numpy as jnp
        import numpy as np
        N = 20000
        E = 5000
        H = 4
        C = 128
        IN = 512
        NEG_SLOPE = 0.2

        def _gatv2(x, src, dst, Wl, bl, Wr, br, att, bias):
            xl = (x @ Wl + bl).reshape(N, H, C)
            xr = (x @ Wr + br).reshape(N, H, C)
            e = jax.nn.leaky_relu(xl[src] + xr[dst], NEG_SLOPE)
            logits = jnp.einsum('ehc,hc->eh', e, att)
            m = jax.ops.segment_max(logits, dst, num_segments=N)
            p = jnp.exp(logits - m[dst])
            s = jax.ops.segment_sum(p, dst, num_segments=N)
            alpha = p / s[dst]
            out = jax.ops.segment_sum(xl[src] * alpha[..., None], dst, num_segments=N)
            return out.reshape(N, H * C) + bias
        key = jax.random.key(seed)
        ks = jax.random.split(key, 16)
        inp = {}
        inp['x'] = jax.random.normal(ks[0], (N, IN), dtype=jnp.float32)
        inp['edge_index'] = jax.random.randint(ks[1], (2, E), 0, N, dtype=jnp.int64)
        in_dims = [IN, H * C]
        k = 2
        for l, d in enumerate(in_dims):
            s = 1.0 / np.sqrt(d)
            inp[f'Wl{l}'] = jax.random.normal(ks[k], (d, H * C), jnp.float32) * s
            k += 1
            inp[f'bl{l}'] = jnp.zeros((H * C,), jnp.float32)
            inp[f'Wr{l}'] = jax.random.normal(ks[k], (d, H * C), jnp.float32) * s
            k += 1
            inp[f'br{l}'] = jnp.zeros((H * C,), jnp.float32)
            inp[f'att{l}'] = jax.random.normal(ks[k], (H, C), jnp.float32) * (1.0 / np.sqrt(C))
            k += 1
            inp[f'bias{l}'] = jnp.zeros((H * C,), jnp.float32)
        return inp
    _L0_gnn_all = _L0_gnn_setup()
    _L0_gnn_in = {k: v for k, v in _L0_gnn_all.items() if k in ('Wl0', 'bl0', 'Wr0', 'br0', 'att0', 'bias0', 'Wl1', 'bl1', 'Wr1', 'br1', 'att1', 'bias1')}
    del _L0_gnn_all

    def _L0_ffn_setup():
        import jax, jax.numpy as jnp
        import numpy as np
        B, S, D, F, E = (8, 64, 512, 32, 8)
        INIT_LAMBDA = 0.2
        LN_EPS = 1e-05
        LN_MERGE = 0.03
        key = jax.random.key(seed)
        ks = jax.random.split(key, 12)
        n = lambda k, shp, s=1.0: jax.random.normal(k, shp, dtype=jnp.float32) * s
        return {'hidden_states': n(ks[0], (B, S, D)), 'gfc1_w': n(ks[1], (D, D), 0.01), 'gfc1_b': jnp.zeros((D,), jnp.float32), 'gfc2_w': n(ks[2], (E, D), 0.01), 'gfc2_b': jnp.full((E,), INIT_LAMBDA, dtype=jnp.float32), 'W1': n(ks[3], (F, D), 0.02), 'b1': jnp.zeros((F,), jnp.float32), 'W2': n(ks[4], (D, F), 0.02), 'b2': jnp.zeros((D,), jnp.float32), 'ln_g': jnp.ones((D,), jnp.float32), 'ln_b': jnp.zeros((D,), jnp.float32), 'tv_W1': n(ks[5], (E, F, D), 0.02), 'tv_b1': n(ks[6], (E, F), 0.02), 'tv_W2': n(ks[7], (E, D, F), 0.02), 'tv_b2': n(ks[8], (E, D), 0.02), 'tv_ln_g': n(ks[9], (E, D), 0.02), 'tv_ln_b': n(ks[10], (E, D), 0.02)}
    _L0_ffn_all = _L0_ffn_setup()
    _L0_ffn_in = {k: v for k, v in _L0_ffn_all.items() if k in ('gfc1_w', 'gfc1_b', 'gfc2_w', 'gfc2_b', 'W1', 'b1', 'W2', 'b2', 'ln_g', 'ln_b', 'tv_W1', 'tv_b1', 'tv_W2', 'tv_b2', 'tv_ln_g', 'tv_ln_b')}
    del _L0_ffn_all
    return {'x': x, 'src': src, 'dst': dst, 'L0_gnn_Wl0': _L0_gnn_in['Wl0'], 'L0_gnn_bl0': _L0_gnn_in['bl0'], 'L0_gnn_Wr0': _L0_gnn_in['Wr0'], 'L0_gnn_br0': _L0_gnn_in['br0'], 'L0_gnn_att0': _L0_gnn_in['att0'], 'L0_gnn_bias0': _L0_gnn_in['bias0'], 'L0_gnn_Wl1': _L0_gnn_in['Wl1'], 'L0_gnn_bl1': _L0_gnn_in['bl1'], 'L0_gnn_Wr1': _L0_gnn_in['Wr1'], 'L0_gnn_br1': _L0_gnn_in['br1'], 'L0_gnn_att1': _L0_gnn_in['att1'], 'L0_gnn_bias1': _L0_gnn_in['bias1'], 'L0_ffn_gfc1_w': _L0_ffn_in['gfc1_w'], 'L0_ffn_gfc1_b': _L0_ffn_in['gfc1_b'], 'L0_ffn_gfc2_w': _L0_ffn_in['gfc2_w'], 'L0_ffn_gfc2_b': _L0_ffn_in['gfc2_b'], 'L0_ffn_W1': _L0_ffn_in['W1'], 'L0_ffn_b1': _L0_ffn_in['b1'], 'L0_ffn_W2': _L0_ffn_in['W2'], 'L0_ffn_b2': _L0_ffn_in['b2'], 'L0_ffn_ln_g': _L0_ffn_in['ln_g'], 'L0_ffn_ln_b': _L0_ffn_in['ln_b'], 'L0_ffn_tv_W1': _L0_ffn_in['tv_W1'], 'L0_ffn_tv_b1': _L0_ffn_in['tv_b1'], 'L0_ffn_tv_W2': _L0_ffn_in['tv_W2'], 'L0_ffn_tv_b2': _L0_ffn_in['tv_b2'], 'L0_ffn_tv_ln_g': _L0_ffn_in['tv_ln_g'], 'L0_ffn_tv_ln_b': _L0_ffn_in['tv_ln_b']}

def reference(x, src, dst, L0_gnn_Wl0, L0_gnn_bl0, L0_gnn_Wr0, L0_gnn_br0, L0_gnn_att0, L0_gnn_bias0, L0_gnn_Wl1, L0_gnn_bl1, L0_gnn_Wr1, L0_gnn_br1, L0_gnn_att1, L0_gnn_bias1, L0_ffn_gfc1_w, L0_ffn_gfc1_b, L0_ffn_gfc2_w, L0_ffn_gfc2_b, L0_ffn_W1, L0_ffn_b1, L0_ffn_W2, L0_ffn_b2, L0_ffn_ln_g, L0_ffn_ln_b, L0_ffn_tv_W1, L0_ffn_tv_b1, L0_ffn_tv_W2, L0_ffn_tv_b2, L0_ffn_tv_ln_g, L0_ffn_tv_ln_b):
    import jax
    import jax.numpy as jnp

    def _L0_gnn_ref(x, edge_index, Wl0, bl0, Wr0, br0, att0, bias0, Wl1, bl1, Wr1, br1, att1, bias1):
        import jax, jax.numpy as jnp
        import numpy as np
        N = 20000
        E = 5000
        H = 4
        C = 128
        IN = 512
        NEG_SLOPE = 0.2

        def _gatv2(x, src, dst, Wl, bl, Wr, br, att, bias):
            xl = (x @ Wl + bl).reshape(N, H, C)
            xr = (x @ Wr + br).reshape(N, H, C)
            e = jax.nn.leaky_relu(xl[src] + xr[dst], NEG_SLOPE)
            logits = jnp.einsum('ehc,hc->eh', e, att)
            m = jax.ops.segment_max(logits, dst, num_segments=N)
            p = jnp.exp(logits - m[dst])
            s = jax.ops.segment_sum(p, dst, num_segments=N)
            alpha = p / s[dst]
            out = jax.ops.segment_sum(xl[src] * alpha[..., None], dst, num_segments=N)
            return out.reshape(N, H * C) + bias
        loops = jnp.arange(N, dtype=edge_index.dtype)
        src = jnp.concatenate([edge_index[0], loops])
        dst = jnp.concatenate([edge_index[1], loops])
        h = _gatv2(x, src, dst, Wl0, bl0, Wr0, br0, att0, bias0)
        h = jax.nn.elu(h)
        h = _gatv2(h, src, dst, Wl1, bl1, Wr1, br1, att1, bias1)
        return h

    def _L0_ffn_ref(hidden_states, gfc1_w, gfc1_b, gfc2_w, gfc2_b, W1, b1, W2, b2, ln_g, ln_b, tv_W1, tv_b1, tv_W2, tv_b2, tv_ln_g, tv_ln_b):
        import jax, jax.numpy as jnp
        import numpy as np
        B, S, D, F, E = (8, 64, 512, 32, 8)
        INIT_LAMBDA = 0.2
        LN_EPS = 1e-05
        LN_MERGE = 0.03
        x = hidden_states
        gh = jax.nn.relu(jnp.einsum('bsd,hd->bsh', x, gfc1_w) + gfc1_b)
        g = (jnp.einsum('bsh,eh->bse', gh, gfc2_w) + gfc2_b).mean(axis=1)
        W1m = W1 + jnp.einsum('be,efd->bfd', g, tv_W1)
        b1m = b1 + g @ tv_b1
        W2m = W2 + jnp.einsum('be,edf->bdf', g, tv_W2)
        b2m = b2 + g @ tv_b2
        lng = ln_g + LN_MERGE * (tv_ln_g - ln_g).sum(axis=0)
        lnb = ln_b + LN_MERGE * (tv_ln_b - ln_b).sum(axis=0)
        h = jax.nn.relu(jnp.einsum('bsd,bfd->bsf', x, W1m) + b1m[:, None, :])
        out = jnp.einsum('bsf,bdf->bsd', h, W2m) + b2m[:, None, :]
        res = x + out
        mu = res.mean(axis=-1, keepdims=True)
        var = res.var(axis=-1, keepdims=True)
        return (res - mu) * jax.lax.rsqrt(var + LN_EPS) * lng + lnb
    edge_index = jnp.stack([src, dst])
    x = x + _L0_gnn_ref(_layernorm(x, axis=-1), edge_index, L0_gnn_Wl0, L0_gnn_bl0, L0_gnn_Wr0, L0_gnn_br0, L0_gnn_att0, L0_gnn_bias0, L0_gnn_Wl1, L0_gnn_bl1, L0_gnn_Wr1, L0_gnn_br1, L0_gnn_att1, L0_gnn_bias1)
    x = x + _L0_ffn_ref(_layernorm(x, axis=-1)[None], L0_ffn_gfc1_w, L0_ffn_gfc1_b, L0_ffn_gfc2_w, L0_ffn_gfc2_b, L0_ffn_W1, L0_ffn_b1, L0_ffn_W2, L0_ffn_b2, L0_ffn_ln_g, L0_ffn_ln_b, L0_ffn_tv_W1, L0_ffn_tv_b1, L0_ffn_tv_W2, L0_ffn_tv_b2, L0_ffn_tv_ln_g, L0_ffn_tv_ln_b)[0]
    return x

_drawn_inputs = setup_inputs


def setup_inputs(seed=0):
    import zlib

    import numpy as np

    out = dict(_drawn_inputs(seed))
    spreads = {'L0_gnn_bl0': (0.0, 0.1),
     'L0_gnn_br0': (0.0, 2.0),
     'L0_gnn_bias0': (0.0, 0.1),
     'L0_gnn_bl1': (0.0, 0.1),
     'L0_gnn_br1': (0.0, 2.0),
     'L0_gnn_bias1': (0.0, 0.1),
     'L0_ffn_gfc1_b': (0.0, 0.8),
     'L0_ffn_gfc2_b': (0.20000000298023224, 0.6),
     'L0_ffn_b1': (0.0, 0.8),
     'L0_ffn_b2': (0.0, 2.0),
     'L0_ffn_ln_g': (1.0, 0.2),
     'L0_ffn_ln_b': (0.0, 0.1)}
    factors = {'L0_gnn_Wr1': 11.566,
     'L0_ffn_gfc1_w': 8.0,
     'L0_ffn_gfc2_w': 8.0,
     'L0_ffn_W1': 3.723,
     'L0_ffn_W2': 2.892,
     'L0_ffn_tv_W1': 5.882,
     'L0_ffn_tv_b1': 8.0,
     'L0_ffn_tv_W2': 5.395,
     'L0_ffn_tv_b2': 28.627,
     'L0_ffn_tv_ln_g': 47.507,
     'L0_ffn_tv_ln_b': 52.085,
     'L0_gnn_Wr0': 2.749}
    for name, (base, spread) in spreads.items():
        noise = np.random.default_rng([zlib.crc32(name.encode()), seed]).standard_normal(out[name].shape)
        drawn = base * np.exp(spread * noise) if base else spread * noise
        out[name] = jnp.asarray(drawn.astype(out[name].dtype))
    for name, factor in factors.items():
        out[name] = (out[name] * factor).astype(out[name].dtype)
    return out
```

```python
import numpy as np
from contextlib import ExitStack
import concourse.bass as bass
from concourse import mybir

F32 = mybir.dt.float32
F32R = mybir.dt.float32r
BF16 = mybir.dt.bfloat16
I32 = mybir.dt.int32
U32 = mybir.dt.uint32
ALU = mybir.AluOpType
ACT = mybir.ActivationFunctionType
AX = mybir.AxisListType

P = 128
U = 6
LEAD = U
D = 512
H = 4
C = D // H
KC = D // P
SW = D + 2 * H
F = 32
NE = 8
SLOPE = 0.2
EPS = 1e-5
MERGE = 0.03
BIG = 1e30
SKIP = 32768.0


class Tile:

    def __init__(self, i, u, rows):
        self.i, self.u, self.rows = i, u, rows
        self.t = i * U + u
        self.t_b = u % 2

    def ready(self):
        return self.t + (LEAD + 1)

    def before(self, n):
        return self.t + (LEAD + 1 - n)


def run_tiles(eng, n_rows, steps, peel=0):
    full, rest = divmod(n_rows, P)
    n = full + (rest > 0)
    most = max(a for _, a in steps)
    loops = (full - most - peel) // U

    def static(t):
        return Tile(t // U, t % U, P if t < full else rest)

    for k in range(most):
        for step, ahead in steps:
            if k >= most - ahead:
                step(static(k - (most - ahead)))
    for t in range(peel):
        for step, ahead in steps:
            step(static(t + ahead))
    with eng.Fori(0, loops) as i:
        for u in range(U):
            for step, ahead in steps:
                step(Tile(i + (u + peel + ahead) // U, (u + peel + ahead) % U, P))
    for t in range(peel + loops * U, n):
        for step, ahead in steps:
            if t + ahead < n:
                step(static(t + ahead))


def build(nc, x, src, dst, w, out):
    N, E = x.shape[0], src.shape[0]
    n_tiles = -(-N // P)
    e_full, e_rest = divmod(E, P)
    e_tiles = e_full + (e_rest > 0)
    ctx = ExitStack()

    def sb(name, shape, dt=F32):
        return ctx.enter_context(nc.sbuf_tensor(name, shape, dt))

    xl_table = nc.dram_tensor("xl_table", [N, D], F32, kind="Internal")
    xr_table = nc.dram_tensor("xr_table", [N, D], F32, kind="Internal")
    state = nc.dram_tensor("state", [N, SW], F32, kind="Internal")
    x1_table = nc.dram_tensor("x1_table", [N, D], F32, kind="Internal")

    with ctx:
        vectors = {k: sb("v_" + k, [P, D]) for k in
                   ("bl0", "br0", "bias0", "att0", "bl1", "br1", "bias1", "att1", "ln_g", "ln_b")}
        ident = sb("ident", [P, P])
        ident16 = sb("ident16", [P, P], BF16)
        earlier = sb("earlier", [P, P])
        ones = sb("ones", [P, 1])
        head_rows = sb("head_rows", [H, H, P])
        eps = sb("eps", [P, 1])
        unit_bias = sb("unit_bias", [33, D], F32R)
        bias_ones = sb("bias_ones", [33, P], F32R)
        src_i = sb("src_i", [P, e_tiles], I32)
        dst_i = sb("dst_i", [P, e_tiles], I32)
        dst_f = sb("dst_f", [P, e_tiles])
        moments = sb("moments", [P, n_tiles, 2])
        unit_sum = sb("unit_sum", [P, D])
        w1m = sb("w1m", [P, KC, F])
        w2m = sb("w2m", [F + 1, D])
        b1m = sb("b1m", [F, 1])
        hidden = sb("hidden", [F + 1, 3, P])
        wraw = sb("wraw", [P, 2, KC, D])
        whi = sb("whi", [P, 2, KC, D], F32R)
        wlo = sb("wlo", [P, 2, KC, D], F32R)

        xin = sb("xin", [P, U, D])
        sin = sb("sin", [P, U, SW])
        xlS = sb("xlS", [P, U, SW])
        xrS = sb("xrS", [P, U, D])
        nrm = sb("nrm", [P, 2, D])
        hiT = sb("hiT", [P, 2, KC, P], F32R)
        loT = sb("loT", [P, 2, KC, P], F32R)
        za = sb("za", [P, 2, D])
        zb = sb("zb", [P, 2, D])
        zc = sb("zc", [P, 2, D])
        scr = sb("scr", [P, 2, D])
        mn = sb("mn", [P, 2, D])
        st6 = sb("st6", [P, 2, 6])
        mv = sb("mv", [P, 2, 2])
        rs4 = sb("rs4", [P, 2, H])
        banks = [ctx.enter_context(nc.psum_tensor(f"bank{i}", [P, D], F32)) for i in range(8)]

        rows_gathered = [ctx.enter_context(nc.semaphore(f"rows_gathered{u}")) for u in range(U)]
        state_gathered = [ctx.enter_context(nc.semaphore(f"state_gathered{b}")) for b in range(2)]
        state_scattered = ctx.enter_context(nc.semaphore("state_scattered"))

        g = dict(N=N, E=E, n_tiles=n_tiles, e_full=e_full, e_rest=e_rest, e_tiles=e_tiles, w=w,
                 xl_table=xl_table, xr_table=xr_table, state=state, x1_table=x1_table, wraw=wraw, whi=whi, wlo=wlo,
                 vectors=vectors, ident=ident, eps=eps, earlier=earlier, head_rows=head_rows, ident16=ident16,
                 unit_bias=unit_bias, bias_ones=bias_ones, src_i=src_i, dst_i=dst_i, dst_f=dst_f, ones=ones,
                 moments=moments, unit_sum=unit_sum, w1m=w1m, w2m=w2m, b1m=b1m, hidden=hidden,
                 xin=xin, sin=sin, nrm=nrm, hiT=hiT, loT=loT, xlS=xlS, xrS=xrS, za=za, zb=zb, zc=zc, scr=scr, mn=mn,
                 st6=st6, mv=mv, rs4=rs4, banks=banks, rows_gathered=rows_gathered,
                 state_gathered=state_gathered, state_scattered=state_scattered)
        constants(nc, src, dst, w, g)
        for layer in range(2):
            transform(nc, layer, x, g)
            edge_pass(nc, layer, g)
        gate(nc, x, g)
        merge(nc, w, g)
        ffn(nc, out, g)


def clear(nc, semaphores):
    with nc.Block() as block:
        @block.gpsimd
        def _(pool):
            for q in semaphores:
                pool.sem_clear(q)


def phase_semaphores(nc, c, name, products, slots=()):
    s = {p: c.enter_context(nc.semaphore(f"{name}_{p}")) for p in products.split()}
    for p in slots:
        s[p] = [c.enter_context(nc.semaphore(f"{name}_{p}{u}")) for u in range(U)]
    c.callback(lambda: clear(nc, [q for v in s.values() for q in (v if type(v) is list else [v])]))
    return s


def lead(pool, s):
    for v in s.values():
        if type(v) is not list:
            pool.sem_inc(v, LEAD)


def bcast(row):
    return row.rearrange("(a d) -> a d", a=1).to_broadcast([P, row.shape[0]])


def load_weights(sp, g, names, sem):
    for n, k in enumerate(names):
        sp.dma_start(g["wraw"][:, n, :, :], g["w"][k].rearrange("(c p) n -> p c n", p=P)).then_inc(sem, 16)


def split_high(act, g, names, loaded, done):
    n = len(names)
    act.wait_ge(loaded, 16 * n)
    act.copy(g["whi"][:, 0:n, :, :], g["wraw"][:, 0:n, :, :]).then_inc(done, 1)


def split_low(dve, g, names, high, done):
    n = len(names)
    dve.wait_ge(high, 1)
    dve.tensor_tensor(g["wlo"][:, 0:n, :, :], g["wraw"][:, 0:n, :, :], g["whi"][:, 0:n, :, :].bitcast(F32),
                      ALU.subtract).then_inc(done, 1)
    dve.wait_ge(done, 1)


def multiply_split(pe, g, ps, b, n, r, more=False):
    for c in range(KC):
        hi, lo = g["hiT"][:, b, c, 0:r], g["loT"][:, b, c, 0:r]
        pe.matmul(ps[0:r, :], hi, g["whi"][:, n, c, :], start=(c == 0), stop=False)
        pe.matmul(ps[0:r, :], hi, g["wlo"][:, n, c, :], start=False, stop=False)
        last = pe.matmul(ps[0:r, :], lo, g["whi"][:, n, c, :], start=False, stop=(c == KC - 1 and not more))
    return last


def constants(nc, src, dst, w, g):
    vectors = g["vectors"]
    e_full, e_rest, E = g["e_full"], g["e_rest"], src.shape[0]
    ident, earlier, head_rows, unit_bias = g["ident"], g["earlier"], g["head_rows"], g["unit_bias"]
    src_i, dst_i, dst_f = g["src_i"], g["dst_i"], g["dst_f"]
    half = NE // 2
    tv = {"ln_g": g["xin"][:, 0:half, :], "ln_b": g["xlS"][:, 0:half, 0:D]}
    part = {"ln_g": g["za"], "ln_b": g["zb"]}
    first = ("Wl0", "Wr0")
    with ExitStack() as c:
        loaded, edges_loaded, rows_loaded, bias_loaded, w_loaded, w_high, w_low, built, zeroed, chain, read = own = [
            c.enter_context(nc.semaphore(n)) for n in
            ("constants_loaded", "edges_loaded", "task_rows_loaded", "unit_bias_loaded", "w_loaded", "w_high", "w_low",
             "masks_built", "masks_zeroed", "layer_norm_merged", "task_rows_read")]
        c.callback(lambda: clear(nc, own))
        block = c.enter_context(nc.Block())

        @block.sync
        def _(sp):
            load_weights(sp, g, first, w_loaded)
            for k, t in vectors.items():
                sp.dma_start(t[:, :], bcast(w[k])).then_inc(loaded, 16)
            for row in (0, 32):
                sp.dma_start(g["scr"][row:row + 1, 0, :], w["gfc1_b"].rearrange("(a d) -> a d", a=1)).then_inc(bias_loaded, 16)
            sp.wait_ge(loaded, 16 * len(vectors))

        @block.scalar
        def _(act):
            act.dma_start(src_i[:, 0:e_full], src[0:e_full * P].rearrange("(p t) -> p t", p=P)).then_inc(edges_loaded, 16)
            act.dma_start(dst_i[:, 0:e_full], dst[0:e_full * P].rearrange("(p t) -> p t", p=P)).then_inc(edges_loaded, 16)
            if e_rest:
                act.dma_start(src_i[0:e_rest, e_full:e_full + 1],
                              src[e_full * P:E].rearrange("(p t) -> p t", t=1)).then_inc(edges_loaded, 16)
                act.dma_start(dst_i[0:e_rest, e_full:e_full + 1],
                              dst[e_full * P:E].rearrange("(p t) -> p t", t=1)).then_inc(edges_loaded, 16)
            for r in range(2):
                if r:
                    act.wait_ge(read, 1)
                for k in ("ln_g", "ln_b"):
                    act.dma_start(tv[k], w["tv_" + k][r * half:(r + 1) * half, :].rearrange("(a e) d -> a e d", a=1)
                                  .to_broadcast([P, half, D])).then_inc(rows_loaded, 16)
                if r == 0:
                    split_high(act, g, first, w_loaded, w_high)
            act.wait_ge(rows_loaded, 16 * 4)

        @block.gpsimd
        def _(pool):
            pool.memset(ident[:, :], 1.0).then_inc(zeroed, 1)
            pool.memset(earlier[:, :], 1.0).then_inc(zeroed, 1)
            pool.memset(head_rows[:, :, :], 1.0).then_inc(zeroed, 1)
            pool.wait_ge(zeroed, 3)
            pool.affine_select(out=ident[:, :], in_=ident[:, :], compare_op=ALU.is_equal, fill=0.0, base=0,
                               pattern=[[-1, P]], channel_multiplier=1).then_inc(built, 1)
            pool.affine_select(out=earlier[:, :], in_=earlier[:, :], compare_op=ALU.is_gt, fill=0.0, base=0,
                               pattern=[[-1, P]], channel_multiplier=1).then_inc(built, 1)
            pool.affine_select(out=head_rows[:, :, :], in_=head_rows[:, :, :], compare_op=ALU.is_equal, fill=0.0, base=0,
                               pattern=[[-1, H], [0, P]], channel_multiplier=1).then_inc(built, 1)
            pool.wait_ge(built, 3)

        @block.vector
        def _(dve):
            dve.memset(g["eps"][:, :], EPS)
            dve.memset(g["ones"][:, :], 1.0)
            dve.memset(g["hidden"][F:F + 1, :, :], 1.0)
            dve.memset(g["unit_sum"][:, :], 0.0)
            dve.memset(g["sin"][:, :, :], 0.0)
            dve.memset(unit_bias[:, :].bitcast(F32), 0.0).then_inc(chain, 1)
            dve.memset(g["bias_ones"][:, :].bitcast(F32), 0.0).then_inc(chain, 1)
            dve.wait_ge(chain, 2)
            for row in (0, 32):
                dve.memset(g["bias_ones"][row:row + 1, :].bitcast(F32), 1.0)
            dve.wait_ge(built, 3)
            dve.tensor_copy(g["ident16"][:, :], ident[:, :])
            dve.wait_ge(edges_loaded, 16 * (4 if e_rest else 2))
            dve.tensor_copy(dst_f[:, 0:e_full], dst_i[:, 0:e_full])
            if e_rest:
                dve.tensor_copy(dst_f[0:e_rest, e_full:e_full + 1], dst_i[0:e_rest, e_full:e_full + 1])
            dve.wait_ge(loaded, 16 * len(vectors))
            dve.wait_ge(bias_loaded, 32)
            n = 3
            dve.tensor_copy(unit_bias[0:1, :], g["scr"][0:1, 0, :]).then_inc(chain, 1)
            dve.wait_ge(chain, n)
            dve.tensor_copy(unit_bias[32:33, :], g["scr"][32:33, 0, :]).then_inc(chain, 1)
            dve.wait_ge(chain, n + 1)
            dve.tensor_tensor(unit_bias[32:33, :], g["scr"][32:33, 0, :], unit_bias[32:33, :].bitcast(F32),
                              ALU.subtract).then_inc(chain, 1)
            n += 2
            for r in range(2):
                dve.wait_ge(rows_loaded, 16 * 2 * (r + 1))
                for k in ("ln_g", "ln_b"):
                    for e in range(half):
                        dve.tensor_tensor(tv[k][:, e, :], tv[k][:, e, :], vectors[k][:, :], ALU.subtract).then_inc(chain, 1)
                        n += 1
                        dve.wait_ge(chain, n)
                        if r == 0 and e == 0:
                            dve.tensor_copy(part[k][:, 0, :], tv[k][:, e, :]).then_inc(chain, 1)
                        else:
                            dve.tensor_tensor(part[k][:, 0, :], part[k][:, 0, :], tv[k][:, e, :], ALU.add).then_inc(chain, 1)
                        n += 1
                        dve.wait_ge(chain, n)
                dve.sem_inc(read, 1)
                if r == 0:
                    split_low(dve, g, first, w_high, w_low)
            for k in ("ln_g", "ln_b"):
                dve.scalar_tensor_tensor(vectors[k][:, :], part[k][:, 0, :], MERGE, vectors[k][:, :],
                                         ALU.mult, ALU.add).then_inc(chain, 1)
                n += 1
            dve.wait_ge(chain, n)


def moments_of(dve, sem, k, source, stats, out_mv):
    dve.bn_stats(stats, source).then_inc(sem["stats"], 1)
    dve.wait_ge(sem["stats"], k.ready())
    dve.sem_inc(sem["apart"], 1)
    dve.bn_aggr(out_mv, stats).then_inc(sem["aggregated"], 1)


def deviation(act, sem, k, out_mv, eps):
    act.wait_ge(sem["aggregated"], k.ready())
    act.activation(out_mv[:, 1:2], out_mv[:, 1:2], ACT.Sqrt, bias=eps[0:k.rows, :]).then_inc(sem["scale"], 1)


def normalise(dve, sem, k, source, out_mv, normed):
    dve.wait_ge(sem["scale"], k.ready())
    dve.reciprocal(out_mv[:, 1:2], out_mv[:, 1:2]).then_inc(sem["inverted"], 1)
    dve.wait_ge(sem["inverted"], k.ready())
    return dve.tensor_scalar(normed, source, out_mv[:, 0:1], out_mv[:, 1:2], ALU.subtract, ALU.mult)


def copy_high(act, s, g, k, ps):
    act.wait_ge(s["transposed"], k.ready())
    act.wait_ge(s["multiplied"], k.before(2))
    act.copy(g["hiT"][:, k.t_b, :, 0:k.rows], chunks(ps)[:, :, 0:k.rows]).then_inc(s["high"], 1)


def take_low(dve, s, g, k, ps):
    dve.wait_ge(s["high"], k.ready())
    dve.tensor_tensor(g["loT"][:, k.t_b, :, 0:k.rows], chunks(ps)[:, :, 0:k.rows],
                      g["hiT"][:, k.t_b, :, 0:k.rows].bitcast(F32), ALU.subtract).then_inc(s["low"], 1)


def transpose_tile(pe, s, g, k, ps, source, free):
    r = k.rows
    pe.wait_ge(s["normed"], k.ready())
    pe.wait_ge(s[free], k.before(2))
    for c in range(KC):
        last = pe.transpose(chunks(ps)[:, c, 0:r], source[:, c * P:(c + 1) * P], g["ident"][0:r, 0:r])
    last.then_inc(s["transposed"], 1)


def chunks(ap):
    return ap[:, :].rearrange("p (c n) -> p c n", c=KC)


def heads(ap):
    return ap.rearrange("p (h c) -> p h c", h=H)


def transform(nc, layer, x, g):
    N = g["N"]
    bl, br, att = (g["vectors"][f"{v}{layer}"] for v in ("bl", "br", "att"))
    bias = g["vectors"]["bias0"]
    xin, sin, nrm, xlS, xrS = (g[k] for k in ("xin", "sin", "nrm", "xlS", "xrS"))
    za, zb, zc, scr, mn, st6, mv, rs4 = (g[k] for k in ("za", "zb", "zc", "scr", "mn", "st6", "mv", "rs4"))
    table, xr_table, state, banks = g["xl_table"], g["xr_table"], g["state"], g["banks"]
    psT, psL, psR = banks[0:2], banks[2:4], banks[4:6]
    own = ("stats aggregated scale inverted" if layer == 0 else
           "inverse features negatives exps positives")
    with ExitStack() as c:
        s = phase_semaphores(nc, c, f"t{layer}", own + " apart saved normed transposed high low lmul multiplied "
                             "xl xr z lrelu product logit", ("loaded", "stored"))
        block = c.enter_context(nc.Block())

        @block.gpsimd
        def _(pool):
            lead(pool, s)

            def add(k):
                r, b = k.rows, k.t_b
                pool.wait_ge(s["xl"], k.ready())
                pool.wait_ge(s["xr"], k.ready())
                pool.wait_ge(s["lrelu"], k.before(2))
                pool.tensor_tensor(za[0:r, b, :], xlS[0:r, k.u, 0:D], xrS[0:r, k.u, :], ALU.add).then_inc(s["z"], 1)

            run_tiles(pool, N, [(add, 0)])

        @block.sync
        def _(sp):
            def store(k):
                r = k.rows
                sp.wait_ge(s["xl"], k.ready())
                sp.wait_ge(s["xr"], k.ready())
                sp.dma_start(table[bass.ds(k.t * P, r), :], xlS[0:r, k.u, 0:D]).then_inc(s["stored"][k.u], 16)
                sp.dma_start(xr_table[bass.ds(k.t * P, r), :], xrS[0:r, k.u, :]).then_inc(s["stored"][k.u], 16)
                sp.wait_ge(s["logit"], k.ready())
                sp.dma_start(state[bass.ds(k.t * P, r), :], xlS[0:r, k.u, :]).then_inc(s["stored"][k.u], 16)

            def confirm(k):
                sp.wait_ge(s["stored"][k.u], k.i * 48 + 48)
                sp.sem_inc(s["saved"], 1)

            run_tiles(sp, N, [(store, 1), (confirm, 0)])
            for u in range(U):
                sp.wait_ge(s["stored"][u], 48 * len(range(u, g["n_tiles"], U)))

        @block.vector
        def _(dve):
            dve.memset(xlS[:, :, D:D + H], 1.0)

            def measure(k):
                r, b = k.rows, k.t_b
                dve.wait_ge(s["loaded"][k.u], k.i * 16 + 16)
                dve.wait_ge(s["normed"], k.before(2))
                moments_of(dve, s, k, xin[0:r, k.u, :], st6[0:r, b, :], mv[0:r, b, :])

            def norm(k):
                r, b = k.rows, k.t_b
                dve.wait_ge(s["transposed"], k.before(2))
                normalise(dve, s, k, xin[0:r, k.u, :], mv[0:r, b, :], nrm[0:r, b, :]).then_inc(s["normed"], 1)

            def features(k):
                r, b = k.rows, k.t_b
                dve.wait_ge(s["loaded"][k.u], k.i * 16 + 16)
                dve.reciprocal(rs4[0:r, b, :], sin[0:r, k.u, D:D + H]).then_inc(s["inverse"], 1)
                dve.wait_ge(s["inverse"], k.ready())
                dve.wait_ge(s["normed"], k.before(2))
                for h in range(H):
                    last = dve.scalar_tensor_tensor(scr[0:r, b, h * C:(h + 1) * C], sin[0:r, k.u, h * C:(h + 1) * C],
                                                    rs4[0:r, b, h:h + 1], bias[0:r, h * C:(h + 1) * C],
                                                    ALU.mult, ALU.add)
                last.then_inc(s["features"], 1)

            def elu(k):
                r, b = k.rows, k.t_b
                dve.wait_ge(s["exps"], k.ready())
                dve.wait_ge(s["positives"], k.ready())
                dve.wait_ge(s["transposed"], k.before(2))
                dve.scalar_tensor_tensor(nrm[0:r, b, :], mn[0:r, b, :], -1.0, scr[0:r, b, :],
                                         ALU.add, ALU.add).then_inc(s["normed"], 1)

            def low(k):
                dve.wait_ge(s["multiplied"], k.before(2))
                take_low(dve, s, g, k, psT[k.t_b])

            def evacuate(k):
                r, b = k.rows, k.t_b
                dve.wait_ge(s["saved"], k.before(U))
                dve.wait_ge(s["z"], k.before(U))
                dve.wait_ge(s["lmul"], k.ready())
                dve.tensor_tensor(xlS[0:r, k.u, 0:D], psL[b][0:r, :], bl[0:r, :], ALU.add).then_inc(s["xl"], 1)
                dve.wait_ge(s["multiplied"], k.ready())
                dve.tensor_tensor(xrS[0:r, k.u, :], psR[b][0:r, :], br[0:r, :], ALU.add).then_inc(s["xr"], 1)

            def logit(k):
                r, b = k.rows, k.t_b
                dve.wait_ge(s["z"], k.ready())
                self_logit(dve, s, k, za, zb, zc, att, xlS[0:r, k.u, D + H:SW])

            first = [(measure, 5), (norm, 4)] if layer == 0 else [(features, 5), (elu, 4)]
            run_tiles(dve, N, first + [(low, 3), (evacuate, 1), (logit, 0)])

        @block.scalar
        def _(act):
            def root(k):
                deviation(act, s, k, mv[0:k.rows, k.t_b, :], g["eps"])

            def parts(k):
                r, b = k.rows, k.t_b
                act.wait_ge(s["features"], k.ready())
                act.wait_ge(s["normed"], k.before(2))
                act.activation(mn[0:r, b, :], scr[0:r, b, :], ACT.Relu, scale=-1.0).then_inc(s["negatives"], 1)
                act.wait_ge(s["negatives"], k.ready())
                act.activation(mn[0:r, b, :], mn[0:r, b, :], ACT.Exp, scale=-1.0).then_inc(s["exps"], 1)
                act.activation(scr[0:r, b, :], scr[0:r, b, :], ACT.Relu).then_inc(s["positives"], 1)

            def high(k):
                copy_high(act, s, g, k, psT[k.t_b])

            def load(k):
                r = k.rows
                act.wait_ge(s["normed"] if layer == 0 else s["features"], k.before(U))
                if layer == 0:
                    act.dma_start(xin[0:r, k.u, :], x[bass.ds(k.t * P, r), :]).then_inc(s["loaded"][k.u], 16)
                else:
                    act.dma_start(sin[0:r, k.u, :], state[bass.ds(k.t * P, r), :]).then_inc(s["loaded"][k.u], 16)

            run_tiles(act, N, [(load, 6), (high, 3), (root if layer == 0 else parts, 5)])

        @block.tensor
        def _(pe):
            def transposes(k):
                transpose_tile(pe, s, g, k, psT[k.t_b], nrm[0:k.rows, k.t_b, :], "low")

            def multiply(k):
                r, b = k.rows, k.t_b
                pe.wait_ge(s["low"], k.ready())
                pe.wait_ge(s["xl"], k.before(2))
                multiply_split(pe, g, psL[b], b, 0, r).then_inc(s["lmul"], 1)
                pe.wait_ge(s["xr"], k.before(2))
                multiply_split(pe, g, psR[b], b, 1, r).then_inc(s["multiplied"], 1)

            run_tiles(pe, N, [(transposes, 3), (multiply, 2)])


def self_logit(dve, s, k, za, zb, zc, att, to):
    r, b = k.rows, k.t_b
    dve.wait_ge(s["product"], k.before(2))
    dve.scalar_tensor_tensor(zb[0:r, b, :], za[0:r, b, :], SLOPE, za[0:r, b, :],
                             ALU.mult, ALU.max).then_inc(s["lrelu"], 1)
    dve.wait_ge(s["lrelu"], k.ready())
    dve.wait_ge(s["logit"], k.before(2))
    dve.tensor_tensor(zc[0:r, b, :], zb[0:r, b, :], att[0:r, :], ALU.mult).then_inc(s["product"], 1)
    dve.wait_ge(s["product"], k.ready())
    dve.tensor_reduce(to, heads(zc[0:r, b, :]), AX.X, ALU.add).then_inc(s["logit"], 1)


def edge_pass(nc, layer, g):
    N, E = g["N"], g["E"]
    att = g["vectors"][f"att{layer}"]
    xlG, xrG = g["xin"], g["xrS"]
    old = g["sin"]
    za, zb, zc, nrm = (g[k] for k in ("za", "zb", "zc", "nrm"))
    src_i, dst_i, dst_f = g["src_i"], g["dst_i"], g["dst_f"]
    banks, ident, ident16, earlier, head_rows = (g[k] for k in ("banks", "ident", "ident16", "earlier", "head_rows"))
    table, xr_table, state = g["xl_table"], g["xr_table"], g["state"]
    psF, psO, psB, psL = banks[0], banks[1], banks[2], banks[5]
    psD, psA = ([m[:, c0:c1] for m in banks[6:8]] for c0, c1 in ((0, P), (P, P + 1)))
    psS, psFs = banks[3][:, 0:H], banks[4][:, 0:2 * H]
    rows_gathered, got_state, put_state = g["rows_gathered"], g["state_gathered"], g["state_scattered"]
    rows_base = [layer * 32 * len(range(u, g["e_tiles"], U)) for u in range(U)]
    base = layer * 16 * g["e_tiles"]
    got_base = [layer * 16 * len(range(b, g["e_tiles"], 2)) for b in range(2)]

    def is_first(k):
        return type(k.i) is int and k.t == 0

    following = ("Wl1", "Wr1") if layer == 0 else ("gfc1T",)
    with ExitStack() as c:
        def sb(name, shape, dt=F32):
            return c.enter_context(nc.sbuf_tensor(f"{name}{layer}", shape, dt))

        w_loaded, w_high, w_low = own = [c.enter_context(nc.semaphore(f"{n}{layer}"))
                                         for n in ("next_w_loaded", "next_w_high", "next_w_low")]
        c.callback(lambda: clear(nc, own))
        s = phase_semaphores(nc, c, f"e{layer}", "apart index spread rowT eq duplicates scatter_float scatter z lrelu "
                             "product logit mask logitT rowsT everywhere peak shifted p weighted summed ordered "
                             "first passed passed_any absent fetch_float fetch written forwarded small selected "
                             "folded diffs factors rescaled sums_scaled snew onew")
        srcc = sb("srcc", [P, U, 1], I32)
        dstc = sb("dstc", [P, U, 1], I32)
        putc = sb("putc", [P, U, 1], I32)
        getc = sb("getc", [P, U, 1], I32)
        getf = sb("getf", [P, 2, 1])
        firsts = sb("firsts", [P, U, 1])
        passed = sb("passed", [P, U, P])
        absent = sb("absent", [P, U, 1])
        dstb = sb("dstb", [P, 2, P])
        eq = sb("eq", [P, U, P])
        mask = sb("mask", [P, U, P], BF16)
        tri = sb("tri", [P, 2, P])
        dup = sb("dup", [P, 2, 1])
        putf = sb("putf", [P, 2, 1])
        lg = sb("lg", [P, U, H])
        lgT = sb("lgT", [H, 2, P])
        pk = sb("pk", [P, U, H])
        prob = sb("prob", [P, U, H])
        df = sb("df", [P, 2, 2, H])
        new = sb("new", [P, 2, SW])
        s4 = sb("s4", [P, 2, H])
        block = c.enter_context(nc.Block())

        @block.sync
        def _(sp):
            load_weights(sp, g, following, w_loaded)

        @block.gpsimd
        def _(pool):
            lead(pool, s)

            def gather(k):
                r = k.rows
                pool.wait_ge(s["index"], k.ready())
                pool.wait_ge(s["weighted"], k.before(U))
                pool.wait_ge(s["z"], k.before(U))
                pool.sem_inc(s["apart"], 1)
                pool.indirect_dma_start(xlG[0:r, k.u, :], None, table[:, :],
                                        bass.IndirectOffsetOnAxis(srcc[0:r, k.u, :].bitcast(U32), 0)).then_inc(rows_gathered[k.u], 16)
                pool.indirect_dma_start(xrG[0:r, k.u, :], None, xr_table[:, :],
                                        bass.IndirectOffsetOnAxis(dstc[0:r, k.u, :].bitcast(U32), 0)).then_inc(rows_gathered[k.u], 16)

            def add(k):
                r, b = k.rows, k.t_b
                pool.wait_ge(rows_gathered[k.u], k.i * 32 + (32 + rows_base[k.u]))
                pool.wait_ge(s["lrelu"], k.before(2))
                pool.tensor_tensor(za[0:r, b, :], xlG[0:r, k.u, :], xrG[0:r, k.u, :], ALU.add).then_inc(s["z"], 1)

            def written(t):
                pool.wait_ge(put_state, t * 16 + (16 + base))
                pool.sem_inc(s["written"], 1)

            def fetch(k):
                r = k.rows
                if not (type(k.i) is int and k.t < 2):
                    pool.wait_ge(put_state, (k.t - 2) * 16 + (16 + base))
                pool.wait_ge(s["fetch"], k.ready())
                pool.wait_ge(s["selected"], k.before(U))
                pool.wait_ge(s["rescaled"], k.before(U))
                pool.sem_inc(s["apart"], 1)
                pool.indirect_dma_start(old[0:r, k.u, :], None, state[:, :],
                                        bass.IndirectOffsetOnAxis(getc[0:r, k.u, :].bitcast(U32), 0),
                                        bounds_check=N - 1, oob_is_err=False).then_inc(got_state[k.t_b], 16)

            def put(k):
                r = k.rows
                if not is_first(k):
                    written(k.t - 1)
                pool.wait_ge(s["scatter"], k.ready())
                pool.wait_ge(s["onew"], k.ready())
                pool.wait_ge(s["snew"], k.ready())
                pool.sem_inc(s["apart"], 1)
                pool.indirect_dma_start(state[:, :], bass.IndirectOffsetOnAxis(putc[0:r, k.u, :].bitcast(U32), 0),
                                        new[0:r, k.t_b, :], None, bounds_check=N - 1,
                                        oob_is_err=False).then_inc(put_state, 16)

            run_tiles(pool, E, [(put, 0), (gather, 5), (add, 4), (fetch, 2)], peel=1)
            written(g["e_tiles"] - 1)

        @block.vector
        def _(dve):
            def index(k):
                r = k.rows
                dve.wait_ge(s["z"], k.before(U))
                dve.tensor_copy(srcc[0:r, k.u, :], src_i[0:r, bass.ds(k.t, 1)])
                dve.tensor_copy(dstc[0:r, k.u, :], dst_i[0:r, bass.ds(k.t, 1)]).then_inc(s["index"], 1)

            def equal(k):
                r, b = k.rows, k.t_b
                dve.wait_ge(s["rowT"], k.ready())
                dve.wait_ge(s["summed"], k.before(U))
                dve.wait_ge(s["mask"], k.before(U))
                dve.tensor_scalar(eq[0:r, k.u, 0:r], psD[b][0:r, 0:r], dst_f[0:r, bass.ds(k.t, 1)], None,
                                  ALU.is_equal).then_inc(s["eq"], 1)
                dve.wait_ge(s["forwarded"], k.before(U))
                dve.wait_ge(s["first"], k.before(1))
                if is_first(k):
                    dve.memset(passed[:, k.u, :], 0.0).then_inc(s["passed"], 1)
                else:
                    dve.tensor_scalar(passed[:, k.u, 0:r], psD[b][:, 0:r], dst_f[:, bass.ds(k.t - 1, 1)],
                                      firsts[:, (k.u - 1) % U, :], ALU.is_equal, ALU.mult).then_inc(s["passed"], 1)
                dve.wait_ge(s["eq"], k.ready())
                dve.wait_ge(s["duplicates"], k.before(2))
                dve.tensor_tensor(tri[0:r, b, 0:r], eq[0:r, k.u, 0:r], earlier[0:r, 0:r], ALU.mult).then_inc(s["ordered"], 1)
                dve.wait_ge(s["ordered"], k.ready())
                dve.tensor_reduce(dup[0:r, b, :], tri[0:r, b, 0:r], AX.X, ALU.add).then_inc(s["duplicates"], 1)
                dve.wait_ge(s["duplicates"], k.ready())
                dve.tensor_scalar(putf[0:r, b, :], dup[0:r, b, :], SKIP, dst_f[0:r, bass.ds(k.t, 1)],
                                  ALU.mult, ALU.add).then_inc(s["scatter_float"], 1)
                dve.tensor_scalar(firsts[0:r, k.u, :], dup[0:r, b, :], 0.0, None, ALU.is_equal).then_inc(s["first"], 1)
                dve.wait_ge(s["scatter_float"], k.ready())
                dve.tensor_copy(putc[0:r, k.u, :], putf[0:r, b, :]).then_inc(s["scatter"], 1)

            def route(k):
                r, b = k.rows, k.t_b
                dve.wait_ge(s["passed_any"], k.ready())
                dve.tensor_scalar(getf[0:r, b, :], psA[b][0:r, :], SKIP, dst_f[0:r, bass.ds(k.t, 1)],
                                  ALU.mult, ALU.add).then_inc(s["fetch_float"], 1)
                dve.tensor_scalar(absent[0:r, k.u, :], psA[b][0:r, :], -1.0, 1.0, ALU.mult, ALU.add).then_inc(s["absent"], 1)
                dve.wait_ge(s["fetch_float"], k.ready())
                dve.tensor_copy(getc[0:r, k.u, :], getf[0:r, b, :]).then_inc(s["fetch"], 1)

            def logit(k):
                dve.wait_ge(s["z"], k.ready())
                dve.wait_ge(s["logitT"], k.before(U))
                dve.wait_ge(s["shifted"], k.before(U))
                self_logit(dve, s, k, za, zb, zc, att, lg[0:k.rows, k.u, :])

            def peak(k):
                r, b = k.rows, k.t_b
                dve.wait_ge(s["everywhere"], k.ready())
                dve.tensor_reduce(pk[0:r, k.u, :], heads(psB[0:r, :])[:, :, 0:r], AX.X, ALU.max).then_inc(s["peak"], 1)
                dve.wait_ge(s["peak"], k.ready())
                dve.tensor_tensor(prob[0:r, k.u, :], lg[0:r, k.u, :], pk[0:r, k.u, :], ALU.subtract).then_inc(s["shifted"], 1)

            def fold(k):
                r, b = k.rows, k.t_b
                dve.wait_ge(got_state[b], k.i * (8 * U) + (16 * (k.u // 2) + 16 + got_base[b]))
                if not is_first(k):
                    dve.wait_ge(s["forwarded"], k.ready())
                    dve.scalar_tensor_tensor(old[0:r, k.u, D:SW], old[0:r, k.u, D:SW], absent[0:r, k.u, :],
                                             psFs[0:r, :], ALU.mult, ALU.add).then_inc(s["small"], 1)
                    dve.wait_ge(s["small"], k.ready())
                else:
                    dve.sem_inc(s["small"], 1)
                dve.tensor_tensor(new[0:r, b, D + H:SW], old[0:r, k.u, D + H:SW], pk[0:r, k.u, :], ALU.max).then_inc(s["folded"], 1)
                dve.wait_ge(s["folded"], k.ready())
                dve.tensor_tensor(df[0:r, b, 0, :], old[0:r, k.u, D + H:SW], new[0:r, b, D + H:SW], ALU.subtract)
                dve.tensor_tensor(df[0:r, b, 1, :], pk[0:r, k.u, :], new[0:r, b, D + H:SW], ALU.subtract).then_inc(s["diffs"], 1)
                if not is_first(k):
                    dve.scalar_tensor_tensor(old[0:r, k.u, 0:D], old[0:r, k.u, 0:D], absent[0:r, k.u, :],
                                             psF[0:r, :], ALU.mult, ALU.add).then_inc(s["selected"], 1)
                else:
                    dve.sem_inc(s["selected"], 1)

            def accumulate(k):
                r, b = k.rows, k.t_b
                dve.wait_ge(s["factors"], k.ready())
                dve.wait_ge(s["summed"], k.ready())
                dve.tensor_tensor(s4[0:r, b, :], psS[0:r, :], df[0:r, b, 1, :], ALU.mult)
                dve.tensor_tensor(new[0:r, b, D:D + H], old[0:r, k.u, D:D + H], df[0:r, b, 0, :], ALU.mult).then_inc(s["sums_scaled"], 1)
                dve.wait_ge(s["sums_scaled"], k.ready())
                dve.tensor_tensor(new[0:r, b, D:D + H], new[0:r, b, D:D + H], s4[0:r, b, :], ALU.add).then_inc(s["snew"], 1)
                dve.wait_ge(s["rescaled"], k.ready())
                for h in range(H):
                    last = dve.scalar_tensor_tensor(new[0:r, b, h * C:(h + 1) * C], psO[0:r, h * C:(h + 1) * C],
                                                    df[0:r, b, 1, h:h + 1], new[0:r, b, h * C:(h + 1) * C],
                                                    ALU.mult, ALU.add)
                last.then_inc(s["onew"], 1)

            run_tiles(dve, E, [(fold, 0), (equal, 4), (route, 3), (accumulate, 0), (logit, 3), (peak, 2), (index, 6)], peel=1)
            split_low(dve, g, following, w_high, w_low)

        @block.scalar
        def _(act):
            def spread(k):
                r, b = k.rows, k.t_b
                act.wait_ge(s["rowT"], k.before(2))
                act.activation(dstb[0:r, b, :], dst_f[0:r, bass.ds(k.t, 1)].to_broadcast([r, P]), ACT.Copy).then_inc(s["spread"], 1)

            def hide(k):
                r = k.rows
                act.wait_ge(s["eq"], k.ready())
                act.wait_ge(s["everywhere"], k.before(U))
                act.activation(mask[0:r, k.u, 0:r], eq[0:r, k.u, 0:r], ACT.Copy, scale=BIG, bias=-BIG).then_inc(s["mask"], 1)

            def transposed_logits(k):
                r, b = k.rows, k.t_b
                act.wait_ge(s["logitT"], k.ready())
                act.wait_ge(s["everywhere"], k.before(2))
                act.copy(lgT[:, b, 0:r], psL[0:H, 0:r]).then_inc(s["rowsT"], 1)

            def weigh(k):
                r, b = k.rows, k.t_b
                act.wait_ge(s["shifted"], k.ready())
                act.activation(prob[0:r, k.u, :], prob[0:r, k.u, :], ACT.Exp).then_inc(s["p"], 1)
                act.wait_ge(s["p"], k.ready())
                act.wait_ge(s["summed"], k.before(2))
                for h in range(H):
                    last = act.activation(nrm[0:r, b, h * C:(h + 1) * C], xlG[0:r, k.u, h * C:(h + 1) * C], ACT.Copy,
                                          scale=prob[0:r, k.u, h:h + 1])
                last.then_inc(s["weighted"], 1)

            def factors(k):
                r, b = k.rows, k.t_b
                act.wait_ge(s["diffs"], k.ready())
                act.activation(df[0:r, b, :, :], df[0:r, b, :, :], ACT.Exp).then_inc(s["factors"], 1)
                act.wait_ge(s["factors"], k.ready())
                act.wait_ge(s["selected"], k.ready())
                for h in range(H):
                    last = act.activation(new[0:r, b, h * C:(h + 1) * C], old[0:r, k.u, h * C:(h + 1) * C], ACT.Copy,
                                          scale=df[0:r, b, 0, h:h + 1])
                last.then_inc(s["rescaled"], 1)

            run_tiles(act, E, [(spread, 5), (factors, 0), (weigh, 1), (hide, 4), (transposed_logits, 3)], peel=1)
            split_high(act, g, following, w_loaded, w_high)

        @block.tensor
        def _(pe):
            def rows(k):
                r, b = k.rows, k.t_b
                pe.wait_ge(s["spread"], k.ready())
                pe.wait_ge(s["eq"], k.before(2))
                pe.wait_ge(s["passed"], k.before(2))
                pe.wait_ge(s["fetch_float"], k.before(2))
                pe.wait_ge(s["absent"], k.before(2))
                pe.transpose(psD[b][:, 0:r], dstb[0:r, b, :], ident[0:r, 0:r]).then_inc(s["rowT"], 1)

            def logits_across(k):
                r, b = k.rows, k.t_b
                pe.wait_ge(s["logit"], k.ready())
                pe.wait_ge(s["rowsT"], k.before(1))
                pe.transpose(psL[0:H, 0:r], lg[0:r, k.u, :], ident[0:r, 0:r]).then_inc(s["logitT"], 1)

            def everywhere(k):
                r, b = k.rows, k.t_b
                pe.wait_ge(s["rowsT"], k.ready())
                pe.wait_ge(s["mask"], k.ready())
                pe.wait_ge(s["peak"], k.before(1))
                pe.matmul(heads(psB[0:r, :])[:, :, 0:r], ident16[0:r, 0:r],
                          mask[0:r, k.u, 0:r].unsqueeze(1).to_broadcast([r, H, r]), start=True, stop=False)
                for h in range(H):
                    last = pe.matmul(psB[0:r, h * P:h * P + r], head_rows[:, h, 0:r], lgT[:, b, 0:r],
                                     start=False, stop=(h == H - 1))
                last.then_inc(s["everywhere"], 1)

            def nodes_passed(k):
                r, b = k.rows, k.t_b
                pe.wait_ge(s["passed"], k.ready())
                pe.matmul(psA[b][0:r, :], passed[:, k.u, 0:r], g["ones"][:, 0:1], start=True, stop=True).then_inc(s["passed_any"], 1)

            def forward(k):
                r, b = k.rows, k.t_b
                if is_first(k):
                    pe.sem_inc(s["forwarded"], 1)
                    return
                pe.wait_ge(s["snew"], k.before(1))
                pe.matmul(psFs[0:r, :], passed[:, k.u, 0:r], new[:, 1 - b, D:SW], start=True, stop=True)
                pe.wait_ge(s["onew"], k.before(1))
                pe.matmul(psF[0:r, :], passed[:, k.u, 0:r], new[:, 1 - b, 0:D], start=True, stop=True).then_inc(s["forwarded"], 1)

            def sums(k):
                r, b = k.rows, k.t_b
                pe.wait_ge(s["weighted"], k.ready())
                pe.wait_ge(s["onew"], k.before(1))
                pe.matmul(psO[0:r, :], eq[0:r, k.u, 0:r], nrm[0:r, b, :], start=True, stop=True)
                pe.matmul(psS[0:r, :], eq[0:r, k.u, 0:r], prob[0:r, k.u, :], start=True, stop=True).then_inc(s["summed"], 1)

            run_tiles(pe, E, [(nodes_passed, 4), (rows, 5), (forward, 1), (sums, 1), (logits_across, 3), (everywhere, 3)], peel=1)


def gate(nc, x, g):
    N = g["N"]
    bias = g["vectors"]["bias1"]
    xin, sin, nrm, x1 = g["xin"], g["sin"], g["nrm"], g["xrS"]
    za, scr, st6, mv, rs4, moments, unit_sum = (g[k] for k in ("za", "scr", "st6", "mv", "rs4", "moments", "unit_sum"))
    banks, state, x1_table = g["banks"], g["state"], g["x1_table"]
    psT, psG = banks[0:2], banks[2:4]
    with ExitStack() as c:
        s = phase_semaphores(nc, c, "g", "apart saved stats aggregated scale inverted inverse biased x1 normed "
                             "transposed high low multiplied units added", ("loaded", "stored"))
        block = c.enter_context(nc.Block())

        @block.gpsimd
        def _(pool):
            lead(pool, s)

            def add_bias(k):
                r, b = k.rows, k.t_b
                pool.wait_ge(s["loaded"][k.u], k.i * 32 + 32)
                pool.wait_ge(s["x1"], k.before(2))
                pool.tensor_tensor(scr[0:r, b, :], xin[0:r, k.u, :], bias[0:r, :], ALU.add).then_inc(s["biased"], 1)

            def accumulate(k):
                r, b = k.rows, k.t_b
                pool.wait_ge(s["units"], k.ready())
                pool.wait_ge(s["added"], k.before(1))
                pool.tensor_tensor(unit_sum[0:r, :], unit_sum[0:r, :], za[0:r, b, :], ALU.add).then_inc(s["added"], 1)

            run_tiles(pool, N, [(add_bias, 6), (accumulate, 1)])

        @block.sync
        def _(sp):
            def store(k):
                r = k.rows
                sp.wait_ge(s["x1"], k.ready())
                sp.dma_start(x1_table[bass.ds(k.t * P, r), :], x1[0:r, k.u, :]).then_inc(s["stored"][k.u], 16)

            def confirm(k):
                sp.wait_ge(s["stored"][k.u], k.i * 16 + 16)
                sp.sem_inc(s["saved"], 1)

            run_tiles(sp, N, [(store, 1), (confirm, 0)])
            for u in range(U):
                sp.wait_ge(s["stored"][u], 16 * len(range(u, g["n_tiles"], U)))

        @block.vector
        def _(dve):
            def residual(k):
                r, b = k.rows, k.t_b
                dve.wait_ge(s["loaded"][k.u], k.i * 32 + 32)
                dve.reciprocal(rs4[0:r, b, :], sin[0:r, k.u, D:D + H]).then_inc(s["inverse"], 1)
                dve.wait_ge(s["inverse"], k.ready())
                dve.wait_ge(s["biased"], k.ready())
                dve.wait_ge(s["saved"], k.before(U))
                for h in range(H):
                    last = dve.scalar_tensor_tensor(x1[0:r, k.u, h * C:(h + 1) * C], sin[0:r, k.u, h * C:(h + 1) * C],
                                                    rs4[0:r, b, h:h + 1], scr[0:r, b, h * C:(h + 1) * C],
                                                    ALU.mult, ALU.add)
                last.then_inc(s["x1"], 1)
                dve.wait_ge(s["x1"], k.ready())
                dve.wait_ge(s["normed"], k.before(2))
                moments_of(dve, s, k, x1[0:r, k.u, :], st6[0:r, b, :], mv[0:r, b, :])

            def norm(k):
                r, b = k.rows, k.t_b
                dve.wait_ge(s["transposed"], k.before(2))
                normalise(dve, s, k, x1[0:r, k.u, :], mv[0:r, b, :], nrm[0:r, b, :])
                dve.tensor_copy(moments[0:r, bass.ds(k.t, 1), :].rearrange("p a b -> p (a b)"),
                                mv[0:r, b, :]).then_inc(s["normed"], 1)

            def low(k):
                dve.wait_ge(s["multiplied"], k.before(2))
                take_low(dve, s, g, k, psT[k.t_b])

            run_tiles(dve, N, [(residual, 5), (norm, 4), (low, 3)])

        @block.scalar
        def _(act):
            def root(k):
                deviation(act, s, k, mv[0:k.rows, k.t_b, :], g["eps"])

            def high(k):
                copy_high(act, s, g, k, psT[k.t_b])

            def units(k):
                r, b = k.rows, k.t_b
                act.wait_ge(s["multiplied"], k.ready())
                act.wait_ge(s["added"], k.before(2))
                act.activation(za[0:r, b, :], psG[b][0:r, :], ACT.Relu).then_inc(s["units"], 1)

            def load(k):
                r = k.rows
                act.wait_ge(s["x1"], k.before(U))
                act.wait_ge(s["biased"], k.before(U))
                act.dma_start(sin[0:r, k.u, :], state[bass.ds(k.t * P, r), :]).then_inc(s["loaded"][k.u], 16)
                act.dma_start(xin[0:r, k.u, :], x[bass.ds(k.t * P, r), :]).then_inc(s["loaded"][k.u], 16)

            run_tiles(act, N, [(load, 6), (root, 5), (high, 3), (units, 1)])

        @block.tensor
        def _(pe):
            def transposes(k):
                transpose_tile(pe, s, g, k, psT[k.t_b], nrm[0:k.rows, k.t_b, :], "low")

            def multiply(k):
                r, b = k.rows, k.t_b
                pe.wait_ge(s["low"], k.ready())
                pe.wait_ge(s["units"], k.before(2))
                multiply_split(pe, g, psG[b], b, 0, r, more=True)
                pe.matmul(psG[b][0:r, :], g["bias_ones"][:, 0:r], g["unit_bias"][:, :],
                          start=False, stop=True).then_inc(s["multiplied"], 1)

            run_tiles(pe, N, [(transposes, 3), (multiply, 2)])


def merge(nc, w, g):
    N = g["N"]
    banks, ones, unit_sum = g["banks"], g["ones"], g["unit_sum"]
    w1m, w2m, b1m = g["w1m"], g["w2m"], g["b1m"]
    with ExitStack() as c:
        def sb(name, shape):
            return c.enter_context(nc.sbuf_tensor(name, shape, F32))

        tv1 = sb("tv1", [P, KC, NE, F])
        tv2 = sb("tv2", [F + 1, NE, D])
        tvb1 = sb("tvb1", [F, NE])
        gfc2T = sb("gfc2T_sb", [P, KC, NE])
        gfc2b = sb("gfc2b_sb", [P, NE])
        mean = sb("mean", [P, KC])
        spread = sb("mean_spread", [P, KC, P])
        gv = sb("gv", [P, NE])
        loaded = c.enter_context(nc.semaphore("merge_loaded"))
        summed = c.enter_context(nc.semaphore("units_summed"))
        spread_s = c.enter_context(nc.semaphore("mean_spread"))
        gated = c.enter_context(nc.semaphore("gate_product"))
        chain = c.enter_context(nc.semaphore("merge_chain"))
        c.callback(lambda: clear(nc, [loaded, summed, spread_s, gated, chain]))
        block = c.enter_context(nc.Block())

        @block.sync
        def _(sp):
            for cc in range(KC):
                sp.dma_start(tv1[:, cc, :, :], w["tv_W1T"][cc * P:(cc + 1) * P, :, :]).then_inc(loaded, 16)
            sp.dma_start(w1m[:, :, :], w["W1T"].rearrange("(c p) f -> p c f", p=P)).then_inc(loaded, 16)
            sp.dma_start(tv2[0:F, :, :], w["tv_W2T"]).then_inc(loaded, 16)
            sp.dma_start(tv2[F:F + 1, :, :], w["tv_b2"].rearrange("(a e) d -> a e d", a=1)).then_inc(loaded, 16)
            sp.dma_start(w2m[0:F, :], w["W2T"]).then_inc(loaded, 16)
            sp.dma_start(w2m[F:F + 1, :], w["b2"].rearrange("(a d) -> a d", a=1)).then_inc(loaded, 16)
            sp.dma_start(tvb1[:, :], w["tv_b1T"]).then_inc(loaded, 16)
            sp.dma_start(b1m[:, :], w["b1"].rearrange("(f a) -> f a", a=1)).then_inc(loaded, 16)
            sp.dma_start(gfc2T[:, :, :], w["gfc2T"].rearrange("(c p) e -> p c e", p=P)).then_inc(loaded, 16)
            sp.dma_start(gfc2b[:, :], bcast(w["gfc2_b"])).then_inc(loaded, 16)
            sp.wait_ge(loaded, 16 * (KC + 9))

        @block.tensor
        def _(pe):
            for cc in range(KC):
                last = pe.matmul(banks[0][:, cc:cc + 1], unit_sum[:, cc * P:(cc + 1) * P], ones[:, 0:1],
                                 start=True, stop=True)
            last.then_inc(summed, 1)
            pe.wait_ge(spread_s, 1)
            pe.wait_ge(loaded, 16 * (KC + 9))
            for cc in range(KC):
                last = pe.matmul(banks[1][:, 0:NE], spread[:, cc, :], gfc2T[:, cc, :],
                                 start=(cc == 0), stop=(cc == KC - 1))
            last.then_inc(gated, 1)

        @block.vector
        def _(dve):
            n = 0

            def link(ins):
                nonlocal n
                n += 1
                ins.then_inc(chain, 1)
                dve.wait_ge(chain, n)

            dve.wait_ge(summed, 1)
            link(dve.tensor_scalar(mean[:, :], banks[0][:, 0:KC], 1.0 / N, None, ALU.mult))
            dve.tensor_copy(spread[:, :, :], mean[:, :].unsqueeze(2).to_broadcast([P, KC, P])).then_inc(spread_s, 1)
            dve.wait_ge(gated, 1)
            link(dve.tensor_tensor(gv[:, :], banks[1][:, 0:NE], gfc2b[:, :], ALU.add))
            dve.wait_ge(loaded, 16 * (KC + 9))
            for e in range(NE):
                for to, tv, r in ((w1m[:, :, :], tv1[:, :, e, :], P), (w2m[:, :], tv2[:, e, :], F + 1),
                                  (b1m[:, :], tvb1[:, e:e + 1], F)):
                    link(dve.scalar_tensor_tensor(to, tv, gv[0:r, e:e + 1], to, ALU.mult, ALU.add))


def ffn(nc, out, g):
    N = g["N"]
    x1, nrm, nrmT = g["xin"], g["xrS"], g["scr"]
    za, zb, zc, outS, st6, moments, mv = (g[k] for k in ("za", "zb", "zc", "xlS", "st6", "moments", "mv"))
    lng, lnb = g["vectors"]["ln_g"], g["vectors"]["ln_b"]
    w1m, w2m, b1m, hidden = g["w1m"], g["w2m"], g["b1m"], g["hidden"]
    banks, ident, x1_table = g["banks"], g["ident"], g["x1_table"]
    psT, psH, psO = banks[0:2], banks[2:4], banks[4:6]
    with ExitStack() as c:
        s = phase_semaphores(nc, c, "f", "apart saved normed transposed featT first hidden second result stats aggregated scale inverted centred "
                   "shift scaled final", ("loaded", "stored"))
        block = c.enter_context(nc.Block())

        @block.gpsimd
        def _(pool):
            lead(pool, s)

            def affine(k):
                r, b = k.rows, k.t_b
                pool.wait_ge(s["loaded"][k.u], k.i * 16 + 16)
                pool.wait_ge(s["final"], k.before(2))
                pool.tensor_tensor(zb[0:r, b, :], x1[0:r, k.u, :], lnb[0:r, :], ALU.add).then_inc(s["shift"], 1)
                pool.wait_ge(s["centred"], k.ready())
                pool.tensor_tensor(zc[0:r, b, :], za[0:r, b, :], lng[0:r, :], ALU.mult).then_inc(s["scaled"], 1)

            run_tiles(pool, N, [(affine, 0)])

        @block.sync
        def _(sp):
            def store(k):
                r = k.rows
                sp.wait_ge(s["final"], k.ready())
                sp.dma_start(out[bass.ds(k.t * P, r), :], outS[0:r, k.u, 0:D]).then_inc(s["stored"][k.u], 16)

            def confirm(k):
                sp.wait_ge(s["stored"][k.u], k.i * 16 + 16)
                sp.sem_inc(s["saved"], 1)

            run_tiles(sp, N, [(store, 1), (confirm, 0)])
            for u in range(U):
                sp.wait_ge(s["stored"][u], 16 * len(range(u, g["n_tiles"], U)))

        @block.vector
        def _(dve):
            def norm(k):
                r = k.rows
                dve.wait_ge(s["loaded"][k.u], k.i * 16 + 16)
                dve.wait_ge(s["result"], k.before(U))
                m = moments[0:r, bass.ds(k.t, 1), :].rearrange("p a b -> p (a b)")
                dve.tensor_scalar(nrm[0:r, k.u, :], x1[0:r, k.u, :], m[:, 0:1], m[:, 1:2],
                                  ALU.subtract, ALU.mult).then_inc(s["normed"], 1)

            def result(k):
                r, b = k.rows, k.t_b
                dve.wait_ge(s["second"], k.ready())
                dve.wait_ge(s["scaled"], k.before(2))
                dve.tensor_tensor(za[0:r, b, :], psO[b][0:r, :], nrm[0:r, k.u, :], ALU.add).then_inc(s["result"], 1)
                dve.wait_ge(s["result"], k.ready())
                moments_of(dve, s, k, za[0:r, b, :], st6[0:r, b, :], mv[0:r, b, :])

            def centre(k):
                r, b = k.rows, k.t_b
                normalise(dve, s, k, za[0:r, b, :], mv[0:r, b, :], za[0:r, b, :]).then_inc(s["centred"], 1)

            def final(k):
                r, b = k.rows, k.t_b
                dve.wait_ge(s["scaled"], k.ready())
                dve.wait_ge(s["shift"], k.ready())
                dve.wait_ge(s["saved"], k.before(U))
                dve.tensor_tensor(outS[0:r, k.u, 0:D], zb[0:r, b, :], zc[0:r, b, :], ALU.add).then_inc(s["final"], 1)

            run_tiles(dve, N, [(norm, 5), (result, 1), (centre, 0), (final, 0)])

        @block.scalar
        def _(act):
            def copy_transposed(k):
                r, b = k.rows, k.t_b
                act.wait_ge(s["transposed"], k.ready())
                act.wait_ge(s["first"], k.before(2))
                act.copy(nrmT[:, b, :].rearrange("p (c n) -> p c n", c=KC)[:, :, 0:r],
                         psT[b][:, :].rearrange("p (c n) -> p c n", c=KC)[:, :, 0:r]).then_inc(s["featT"], 1)

            def units(k):
                r, b = k.rows, k.t_b
                act.wait_ge(s["first"], k.ready())
                act.wait_ge(s["second"], k.before(2))
                act.activation(hidden[0:F, b, 0:r], psH[b][0:F, 0:r], ACT.Relu, bias=b1m[:, 0:1]).then_inc(s["hidden"], 1)

            def spread(k):
                deviation(act, s, k, mv[0:k.rows, k.t_b, :], g["eps"])

            def load(k):
                r = k.rows
                act.wait_ge(s["shift"], k.before(U))
                act.wait_ge(s["normed"], k.before(U))
                act.dma_start(x1[0:r, k.u, :], x1_table[bass.ds(k.t * P, r), :]).then_inc(s["loaded"][k.u], 16)

            run_tiles(act, N, [(load, 6), (copy_transposed, 3), (units, 2), (spread, 1)])

        @block.tensor
        def _(pe):
            def transposes(k):
                r, b = k.rows, k.t_b
                pe.wait_ge(s["normed"], k.ready())
                pe.wait_ge(s["featT"], k.before(2))
                for c in range(KC):
                    last = pe.transpose(psT[b][:, c * P:c * P + r], nrm[0:r, k.u, c * P:(c + 1) * P], ident[0:r, 0:r])
                last.then_inc(s["transposed"], 1)

            def first(k):
                r, b = k.rows, k.t_b
                pe.wait_ge(s["featT"], k.ready())
                pe.wait_ge(s["hidden"], k.before(2))
                for c in range(KC):
                    last = pe.matmul(psH[b][0:F, 0:r], w1m[:, c, :], nrmT[:, b, c * P:c * P + r],
                                     start=(c == 0), stop=(c == KC - 1))
                last.then_inc(s["first"], 1)

            def second(k):
                r, b = k.rows, k.t_b
                pe.wait_ge(s["hidden"], k.ready())
                pe.wait_ge(s["result"], k.before(2))
                pe.matmul(psO[b][0:r, :], hidden[:, b, 0:r], w2m[:, :], start=True, stop=True).then_inc(s["second"], 1)

            run_tiles(pe, N, [(transposes, 4), (first, 3), (second, 2)])


def kernel(**a):
    import concourse.bacc as bacc
    from concourse.bass_utils import run_bass_kernel_spmd

    nc = bacc.Bacc("TRN2", target_bir_lowering=False, num_devices=1)
    flat = {
        "x": a["x"], "src": a["src"], "dst": a["dst"],
        "gfc1T": np.asarray(a["L0_ffn_gfc1_w"]).T, "gfc1_b": a["L0_ffn_gfc1_b"],
        "gfc2T": np.asarray(a["L0_ffn_gfc2_w"]).T, "gfc2_b": a["L0_ffn_gfc2_b"],
        "W1T": np.asarray(a["L0_ffn_W1"]).T, "b1": a["L0_ffn_b1"],
        "W2T": np.asarray(a["L0_ffn_W2"]).T, "b2": a["L0_ffn_b2"],
        "ln_g": a["L0_ffn_ln_g"], "ln_b": a["L0_ffn_ln_b"],
        "tv_W1T": np.asarray(a["L0_ffn_tv_W1"]).transpose(2, 0, 1),
        "tv_b1T": np.asarray(a["L0_ffn_tv_b1"]).T,
        "tv_W2T": np.asarray(a["L0_ffn_tv_W2"]).transpose(2, 0, 1),
        "tv_b2": a["L0_ffn_tv_b2"], "tv_ln_g": a["L0_ffn_tv_ln_g"], "tv_ln_b": a["L0_ffn_tv_ln_b"],
    }
    for v in ("Wl", "bl", "Wr", "br", "bias"):
        for n in range(2):
            flat[f"{v}{n}"] = a[f"L0_gnn_{v}{n}"]
    for n in range(2):
        flat[f"att{n}"] = np.asarray(a[f"L0_gnn_att{n}"]).reshape(-1)
    arrays, w = {}, {}
    for name, v in flat.items():
        v = np.ascontiguousarray(v)
        arrays[f"in_{name}"] = v
        w[name] = nc.dram_tensor(f"in_{name}", v.shape, mybir.dt.from_np(v.dtype), kind="ExternalInput").ap()
    shape = np.asarray(a["x"]).shape
    out = nc.dram_tensor("out", shape, F32, kind="ExternalOutput").ap()
    build(nc, w["x"], w["src"], w["dst"], w, out)
    r = run_bass_kernel_spmd(nc, [arrays], core_ids=[0])
    return r.results[0]["out"]
```

```python
import numpy as np
from contextlib import ExitStack
import concourse.bass as bass
from concourse import mybir

F32 = mybir.dt.float32
F32R = mybir.dt.float32r
BF16 = mybir.dt.bfloat16
I32 = mybir.dt.int32
U32 = mybir.dt.uint32
ALU = mybir.AluOpType
ACT = mybir.ActivationFunctionType
AX = mybir.AxisListType

P = 128
U = 6
LEAD = U
D = 512
H = 4
C = D // H
KC = D // P
SW = D + 2 * H
F = 32
FS = 3 * F + 2
NE = 8
SLOPE = 0.2
EPS = 1e-5
MERGE = 0.03
BIG = 1e30
SKIP = 32768.0


class Tile:

    def __init__(self, i, u, rows):
        self.i, self.u, self.rows = i, u, rows
        self.t = i * U + u
        self.t_b = u % 2

    def ready(self):
        return self.t + (LEAD + 1)

    def before(self, n):
        return self.t + (LEAD + 1 - n)


def run_tiles(eng, n_rows, steps, peel=0):
    full, rest = divmod(n_rows, P)
    n = full + (rest > 0)
    most = max(a for _, a in steps)
    loops = (full - most - peel) // U

    def static(t):
        return Tile(t // U, t % U, P if t < full else rest)

    for k in range(most):
        for step, ahead in steps:
            if k >= most - ahead:
                step(static(k - (most - ahead)))
    for t in range(peel):
        for step, ahead in steps:
            step(static(t + ahead))
    with eng.Fori(0, loops) as i:
        for u in range(U):
            for step, ahead in steps:
                step(Tile(i + (u + peel + ahead) // U, (u + peel + ahead) % U, P))
    for t in range(peel + loops * U, n):
        for step, ahead in steps:
            if t + ahead < n:
                step(static(t + ahead))


def build(nc, x, src, dst, w, out):
    N, E = x.shape[0], src.shape[0]
    n_tiles = -(-N // P)
    e_full, e_rest = divmod(E, P)
    e_tiles = e_full + (e_rest > 0)
    ctx = ExitStack()

    def sb(name, shape, dt=F32):
        return ctx.enter_context(nc.sbuf_tensor(name, shape, dt))

    xl_table = nc.dram_tensor("xl_table", [N, D], F32, kind="Internal")
    xr_table = nc.dram_tensor("xr_table", [N, D], F32, kind="Internal")
    state = nc.dram_tensor("state", [N, SW], F32, kind="Internal")
    x1_table = nc.dram_tensor("x1_table", [N, D], F32, kind="Internal")

    with ctx:
        vectors = {k: sb("v_" + k, [P, D]) for k in
                   ("bl0", "br0", "bias0", "att0", "bl1", "br1", "bias1", "att1")}
        ln_g, ln_b = sb("ln_g", [P, D]), sb("ln_b", [P, D])
        ident = sb("ident", [P, P])
        ident16 = sb("ident16", [P, P], BF16)
        earlier = sb("earlier", [P, P])
        ones = sb("ones", [P, 1])
        head_rows = sb("head_rows", [H, H, P])
        eps = sb("eps", [P, 1])
        unit_bias = sb("unit_bias", [33, D], F32R)
        bias_ones = sb("bias_ones", [33, P], F32R)
        src_i = sb("src_i", [P, e_tiles], I32)
        dst_i = sb("dst_i", [P, e_tiles], I32)
        dst_f = sb("dst_f", [P, e_tiles])
        moments = sb("moments", [P, n_tiles, 2])
        unit_sum = sb("unit_sum", [P, D])
        w1m = sb("w1m", [P, KC, 3, F])
        b1m = sb("b1m", [3 * F, 1])
        w2parts = sb("w2parts", [FS, D], F32R)
        hidden = sb("hidden", [FS, 2, P], F32R)
        wraw = sb("wraw", [P, 2, KC, D])
        whi = sb("whi", [P, 2, KC, D], F32R)
        wlo = sb("wlo", [P, 2, KC, D], F32R)

        xin = sb("xin", [P, U, D])
        sin = sb("sin", [P, U, SW])
        xlS = sb("xlS", [P, U, SW])
        xrS = sb("xrS", [P, U, D])
        nrm = sb("nrm", [P, 2, D])
        hiT = sb("hiT", [P, 2, KC, P], F32R)
        loT = sb("loT", [P, 2, KC, P], F32R)
        za = sb("za", [P, 2, D])
        zb = sb("zb", [P, 2, D])
        zc = sb("zc", [P, 2, D])
        scr = sb("scr", [P, 2, D])
        mn = sb("mn", [P, 2, D])
        st6 = sb("st6", [P, 2, 6])
        mv = sb("mv", [P, 2, 2])
        rs4 = sb("rs4", [P, 2, H])
        banks = [ctx.enter_context(nc.psum_tensor(f"bank{i}", [P, D], F32)) for i in range(8)]

        rows_gathered = [ctx.enter_context(nc.semaphore(f"rows_gathered{u}")) for u in range(U)]
        state_gathered = [ctx.enter_context(nc.semaphore(f"state_gathered{b}")) for b in range(2)]
        state_scattered = ctx.enter_context(nc.semaphore("state_scattered"))

        g = dict(N=N, E=E, n_tiles=n_tiles, e_full=e_full, e_rest=e_rest, e_tiles=e_tiles, w=w,
                 xl_table=xl_table, xr_table=xr_table, state=state, x1_table=x1_table, wraw=wraw, whi=whi, wlo=wlo,
                 vectors=vectors, ln_g=ln_g, ln_b=ln_b, ident=ident, eps=eps, earlier=earlier, head_rows=head_rows, ident16=ident16,
                 unit_bias=unit_bias, bias_ones=bias_ones, src_i=src_i, dst_i=dst_i, dst_f=dst_f, ones=ones,
                 moments=moments, unit_sum=unit_sum, w1m=w1m, w2parts=w2parts, b1m=b1m, hidden=hidden,
                 xin=xin, sin=sin, nrm=nrm, hiT=hiT, loT=loT, xlS=xlS, xrS=xrS, za=za, zb=zb, zc=zc, scr=scr, mn=mn,
                 st6=st6, mv=mv, rs4=rs4, banks=banks, rows_gathered=rows_gathered,
                 state_gathered=state_gathered, state_scattered=state_scattered)
        constants(nc, src, dst, w, g)
        for layer in range(2):
            transform(nc, layer, x, g)
            edge_pass(nc, layer, g)
        with ExitStack() as c:
            inputs = merge_inputs(nc, c, w, g)
            gate(nc, x, g, inputs)
            merge(nc, g, inputs)
        ffn(nc, out, g)


def clear(nc, semaphores):
    with nc.Block() as block:
        @block.gpsimd
        def _(pool):
            for q in semaphores:
                pool.sem_clear(q)


def phase_semaphores(nc, c, name, products, slots=()):
    s = {p: c.enter_context(nc.semaphore(f"{name}_{p}")) for p in products.split()}
    for p in slots:
        s[p] = [c.enter_context(nc.semaphore(f"{name}_{p}{u}")) for u in range(U)]
    c.callback(lambda: clear(nc, [q for v in s.values() for q in (v if type(v) is list else [v])]))
    return s


def lead(pool, s):
    for v in s.values():
        if type(v) is not list:
            pool.sem_inc(v, LEAD)


def bcast(row):
    return row.rearrange("(a d) -> a d", a=1).to_broadcast([P, row.shape[0]])


def load_weights(sp, g, names, sem):
    for n, k in enumerate(names):
        sp.dma_start(g["wraw"][:, n, :, :], g["w"][k].rearrange("(c p) n -> p c n", p=P)).then_inc(sem, 16)


def split_high(act, g, names, loaded, done):
    n = len(names)
    act.wait_ge(loaded, 16 * n)
    act.copy(g["whi"][:, 0:n, :, :], g["wraw"][:, 0:n, :, :]).then_inc(done, 1)


def split_low(dve, g, names, high, done):
    n = len(names)
    dve.wait_ge(high, 1)
    dve.tensor_tensor(g["wlo"][:, 0:n, :, :], g["wraw"][:, 0:n, :, :], g["whi"][:, 0:n, :, :].bitcast(F32),
                      ALU.subtract).then_inc(done, 1)
    dve.wait_ge(done, 1)


def multiply_split(pe, g, ps, b, n, r, more=False):
    for c in range(KC):
        hi, lo = g["hiT"][:, b, c, 0:r], g["loT"][:, b, c, 0:r]
        pe.matmul(ps[0:r, :], hi, g["whi"][:, n, c, :], start=(c == 0), stop=False)
        pe.matmul(ps[0:r, :], hi, g["wlo"][:, n, c, :], start=False, stop=False)
        last = pe.matmul(ps[0:r, :], lo, g["whi"][:, n, c, :], start=False, stop=(c == KC - 1 and not more))
    return last


def constants(nc, src, dst, w, g):
    vectors = g["vectors"]
    e_full, e_rest, E = g["e_full"], g["e_rest"], src.shape[0]
    ident, earlier, head_rows, unit_bias = g["ident"], g["earlier"], g["head_rows"], g["unit_bias"]
    src_i, dst_i, dst_f = g["src_i"], g["dst_i"], g["dst_f"]
    first = ("Wl0", "Wr0")
    with ExitStack() as c:
        loaded, edges_loaded, bias_loaded, w_loaded, w_high, w_low, built, zeroed, chain = own = [
            c.enter_context(nc.semaphore(n)) for n in
            ("constants_loaded", "edges_loaded", "unit_bias_loaded", "w_loaded", "w_high", "w_low",
             "masks_built", "masks_zeroed", "unit_bias_parts")]
        c.callback(lambda: clear(nc, own))
        block = c.enter_context(nc.Block())

        @block.sync
        def _(sp):
            load_weights(sp, g, first, w_loaded)
            for row in (0, 32):
                sp.dma_start(g["scr"][row:row + 1, 0, :], w["gfc1_b"].rearrange("(a d) -> a d", a=1)).then_inc(bias_loaded, 16)
            for k, t in vectors.items():
                sp.dma_start(t[:, :], bcast(w[k])).then_inc(loaded, 16)
            sp.wait_ge(loaded, 16 * len(vectors))

        @block.scalar
        def _(act):
            act.dma_start(src_i[:, 0:e_full], src[0:e_full * P].rearrange("(p t) -> p t", p=P)).then_inc(edges_loaded, 16)
            act.dma_start(dst_i[:, 0:e_full], dst[0:e_full * P].rearrange("(p t) -> p t", p=P)).then_inc(edges_loaded, 16)
            if e_rest:
                act.dma_start(src_i[0:e_rest, e_full:e_full + 1],
                              src[e_full * P:E].rearrange("(p t) -> p t", t=1)).then_inc(edges_loaded, 16)
                act.dma_start(dst_i[0:e_rest, e_full:e_full + 1],
                              dst[e_full * P:E].rearrange("(p t) -> p t", t=1)).then_inc(edges_loaded, 16)
            split_high(act, g, first, w_loaded, w_high)

        @block.gpsimd
        def _(pool):
            pool.memset(ident[:, :], 1.0).then_inc(zeroed, 1)
            pool.memset(earlier[:, :], 1.0).then_inc(zeroed, 1)
            pool.memset(head_rows[:, :, :], 1.0).then_inc(zeroed, 1)
            pool.wait_ge(zeroed, 3)
            pool.affine_select(out=ident[:, :], in_=ident[:, :], compare_op=ALU.is_equal, fill=0.0, base=0,
                               pattern=[[-1, P]], channel_multiplier=1).then_inc(built, 1)
            pool.affine_select(out=earlier[:, :], in_=earlier[:, :], compare_op=ALU.is_gt, fill=0.0, base=0,
                               pattern=[[-1, P]], channel_multiplier=1).then_inc(built, 1)
            pool.affine_select(out=head_rows[:, :, :], in_=head_rows[:, :, :], compare_op=ALU.is_equal, fill=0.0, base=0,
                               pattern=[[-1, H], [0, P]], channel_multiplier=1).then_inc(built, 1)
            pool.wait_ge(built, 3)

        @block.vector
        def _(dve):
            dve.memset(g["eps"][:, :], EPS)
            dve.memset(g["ones"][:, :], 1.0)
            dve.memset(g["hidden"][3 * F:FS, :, :].bitcast(F32), 1.0)
            dve.memset(g["unit_sum"][:, :], 0.0)
            dve.memset(g["sin"][:, :, :], 0.0)
            dve.memset(unit_bias[:, :].bitcast(F32), 0.0).then_inc(chain, 1)
            dve.memset(g["bias_ones"][:, :].bitcast(F32), 0.0).then_inc(chain, 1)
            dve.wait_ge(chain, 2)
            for row in (0, 32):
                dve.memset(g["bias_ones"][row:row + 1, :].bitcast(F32), 1.0)
            dve.wait_ge(built, 3)
            dve.tensor_copy(g["ident16"][:, :], ident[:, :])
            dve.wait_ge(edges_loaded, 16 * (4 if e_rest else 2))
            dve.tensor_copy(dst_f[:, 0:e_full], dst_i[:, 0:e_full])
            if e_rest:
                dve.tensor_copy(dst_f[0:e_rest, e_full:e_full + 1], dst_i[0:e_rest, e_full:e_full + 1])
            split_low(dve, g, first, w_high, w_low)
            dve.wait_ge(bias_loaded, 32)
            n = 3
            dve.tensor_copy(unit_bias[0:1, :], g["scr"][0:1, 0, :]).then_inc(chain, 1)
            dve.wait_ge(chain, n)
            dve.tensor_copy(unit_bias[32:33, :], g["scr"][32:33, 0, :]).then_inc(chain, 1)
            dve.wait_ge(chain, n + 1)
            dve.tensor_tensor(unit_bias[32:33, :], g["scr"][32:33, 0, :], unit_bias[32:33, :].bitcast(F32),
                              ALU.subtract).then_inc(chain, 1)
            dve.wait_ge(chain, n + 2)


def moments_of(dve, sem, k, source, stats, out_mv):
    dve.bn_stats(stats, source).then_inc(sem["stats"], 1)
    dve.wait_ge(sem["stats"], k.ready())
    dve.sem_inc(sem["apart"], 1)
    dve.bn_aggr(out_mv, stats).then_inc(sem["aggregated"], 1)


def deviation(act, sem, k, out_mv, eps):
    act.wait_ge(sem["aggregated"], k.ready())
    act.activation(out_mv[:, 1:2], out_mv[:, 1:2], ACT.Sqrt, bias=eps[0:k.rows, :]).then_inc(sem["scale"], 1)


def normalise(dve, sem, k, source, out_mv, normed):
    dve.wait_ge(sem["scale"], k.ready())
    dve.reciprocal(out_mv[:, 1:2], out_mv[:, 1:2]).then_inc(sem["inverted"], 1)
    dve.wait_ge(sem["inverted"], k.ready())
    return dve.tensor_scalar(normed, source, out_mv[:, 0:1], out_mv[:, 1:2], ALU.subtract, ALU.mult)


def negative_mean(dve, sem, k, out_mv):
    dve.wait_ge(sem["scale"], k.ready())
    dve.reciprocal(out_mv[:, 1:2], out_mv[:, 1:2]).then_inc(sem["inverted"], 1)
    dve.wait_ge(sem["inverted"], k.ready())
    dve.scalar_tensor_tensor(out_mv[:, 0:1], out_mv[:, 0:1], -1.0, out_mv[:, 1:2],
                             ALU.mult, ALU.mult).then_inc(sem["shift"], 1)


def copy_high(act, s, g, k, ps):
    act.wait_ge(s["transposed"], k.ready())
    act.wait_ge(s["multiplied"], k.before(2))
    act.copy(g["hiT"][:, k.t_b, :, 0:k.rows], chunks(ps)[:, :, 0:k.rows]).then_inc(s["high"], 1)


def take_low(dve, s, g, k, ps):
    dve.wait_ge(s["high"], k.ready())
    dve.tensor_tensor(g["loT"][:, k.t_b, :, 0:k.rows], chunks(ps)[:, :, 0:k.rows],
                      g["hiT"][:, k.t_b, :, 0:k.rows].bitcast(F32), ALU.subtract).then_inc(s["low"], 1)


def transpose_tile(pe, s, g, k, ps, source, free):
    r = k.rows
    pe.wait_ge(s["normed"], k.ready())
    pe.wait_ge(s[free], k.before(2))
    for c in range(KC):
        last = pe.transpose(chunks(ps)[:, c, 0:r], source[:, c * P:(c + 1) * P], g["ident"][0:r, 0:r])
    last.then_inc(s["transposed"], 1)


def chunks(ap):
    return ap[:, :].rearrange("p (c n) -> p c n", c=KC)


def heads(ap):
    return ap.rearrange("p (h c) -> p h c", h=H)


def transform(nc, layer, x, g):
    N = g["N"]
    bl, br, att = (g["vectors"][f"{v}{layer}"] for v in ("bl", "br", "att"))
    bias = g["vectors"]["bias0"]
    xin, sin, nrm, xlS, xrS = (g[k] for k in ("xin", "sin", "nrm", "xlS", "xrS"))
    za, zb, zc, scr, mn, st6, mv, rs4 = (g[k] for k in ("za", "zb", "zc", "scr", "mn", "st6", "mv", "rs4"))
    table, xr_table, state, banks = g["xl_table"], g["xr_table"], g["state"], g["banks"]
    psT, psL, psR = banks[0:2], banks[2:4], banks[4:6]
    own = ("stats aggregated scale inverted" if layer == 0 else
           "inverse features negatives exps positives")
    with ExitStack() as c:
        s = phase_semaphores(nc, c, f"t{layer}", own + " apart saved normed transposed high low lmul multiplied "
                             "xl xr z lrelu product logit", ("loaded", "stored"))
        block = c.enter_context(nc.Block())

        @block.gpsimd
        def _(pool):
            lead(pool, s)

            def add(k):
                r, b = k.rows, k.t_b
                pool.wait_ge(s["xl"], k.ready())
                pool.wait_ge(s["xr"], k.ready())
                pool.wait_ge(s["lrelu"], k.before(2))
                pool.tensor_tensor(za[0:r, b, :], xlS[0:r, k.u, 0:D], xrS[0:r, k.u, :], ALU.add).then_inc(s["z"], 1)

            run_tiles(pool, N, [(add, 0)])

        @block.sync
        def _(sp):
            def store(k):
                r = k.rows
                sp.wait_ge(s["xl"], k.ready())
                sp.wait_ge(s["xr"], k.ready())
                sp.dma_start(table[bass.ds(k.t * P, r), :], xlS[0:r, k.u, 0:D]).then_inc(s["stored"][k.u], 16)
                sp.dma_start(xr_table[bass.ds(k.t * P, r), :], xrS[0:r, k.u, :]).then_inc(s["stored"][k.u], 16)
                sp.wait_ge(s["logit"], k.ready())
                sp.dma_start(state[bass.ds(k.t * P, r), :], xlS[0:r, k.u, :]).then_inc(s["stored"][k.u], 16)

            def confirm(k):
                sp.wait_ge(s["stored"][k.u], k.i * 48 + 48)
                sp.sem_inc(s["saved"], 1)

            run_tiles(sp, N, [(store, 1), (confirm, 0)])
            for u in range(U):
                sp.wait_ge(s["stored"][u], 48 * len(range(u, g["n_tiles"], U)))

        @block.vector
        def _(dve):
            dve.memset(xlS[:, :, D:D + H], 1.0)

            def measure(k):
                r, b = k.rows, k.t_b
                dve.wait_ge(s["loaded"][k.u], k.i * 16 + 16)
                dve.wait_ge(s["normed"], k.before(2))
                moments_of(dve, s, k, xin[0:r, k.u, :], st6[0:r, b, :], mv[0:r, b, :])

            def norm(k):
                r, b = k.rows, k.t_b
                dve.wait_ge(s["transposed"], k.before(2))
                normalise(dve, s, k, xin[0:r, k.u, :], mv[0:r, b, :], nrm[0:r, b, :]).then_inc(s["normed"], 1)

            def features(k):
                r, b = k.rows, k.t_b
                dve.wait_ge(s["loaded"][k.u], k.i * 16 + 16)
                dve.reciprocal(rs4[0:r, b, :], sin[0:r, k.u, D:D + H]).then_inc(s["inverse"], 1)
                dve.wait_ge(s["inverse"], k.ready())
                dve.wait_ge(s["normed"], k.before(2))
                for h in range(H):
                    last = dve.scalar_tensor_tensor(scr[0:r, b, h * C:(h + 1) * C], sin[0:r, k.u, h * C:(h + 1) * C],
                                                    rs4[0:r, b, h:h + 1], bias[0:r, h * C:(h + 1) * C],
                                                    ALU.mult, ALU.add)
                last.then_inc(s["features"], 1)

            def elu(k):
                r, b = k.rows, k.t_b
                dve.wait_ge(s["exps"], k.ready())
                dve.wait_ge(s["positives"], k.ready())
                dve.wait_ge(s["transposed"], k.before(2))
                dve.scalar_tensor_tensor(nrm[0:r, b, :], mn[0:r, b, :], -1.0, scr[0:r, b, :],
                                         ALU.add, ALU.add).then_inc(s["normed"], 1)

            def low(k):
                dve.wait_ge(s["multiplied"], k.before(2))
                take_low(dve, s, g, k, psT[k.t_b])

            def evacuate(k):
                r, b = k.rows, k.t_b
                dve.wait_ge(s["saved"], k.before(U))
                dve.wait_ge(s["z"], k.before(U))
                dve.wait_ge(s["lmul"], k.ready())
                dve.tensor_tensor(xlS[0:r, k.u, 0:D], psL[b][0:r, :], bl[0:r, :], ALU.add).then_inc(s["xl"], 1)
                dve.wait_ge(s["multiplied"], k.ready())
                dve.tensor_tensor(xrS[0:r, k.u, :], psR[b][0:r, :], br[0:r, :], ALU.add).then_inc(s["xr"], 1)

            def logit(k):
                r, b = k.rows, k.t_b
                dve.wait_ge(s["z"], k.ready())
                self_logit(dve, s, k, za, zb, zc, att, xlS[0:r, k.u, D + H:SW])

            first = [(measure, 5), (norm, 4)] if layer == 0 else [(features, 5), (elu, 4)]
            run_tiles(dve, N, first + [(low, 3), (evacuate, 1), (logit, 0)])

        @block.scalar
        def _(act):
            def root(k):
                deviation(act, s, k, mv[0:k.rows, k.t_b, :], g["eps"])

            def parts(k):
                r, b = k.rows, k.t_b
                act.wait_ge(s["features"], k.ready())
                act.wait_ge(s["normed"], k.before(2))
                act.activation(mn[0:r, b, :], scr[0:r, b, :], ACT.Relu, scale=-1.0).then_inc(s["negatives"], 1)
                act.wait_ge(s["negatives"], k.ready())
                act.activation(mn[0:r, b, :], mn[0:r, b, :], ACT.Exp, scale=-1.0).then_inc(s["exps"], 1)
                act.activation(scr[0:r, b, :], scr[0:r, b, :], ACT.Relu).then_inc(s["positives"], 1)

            def high(k):
                copy_high(act, s, g, k, psT[k.t_b])

            def load(k):
                r = k.rows
                act.wait_ge(s["normed"] if layer == 0 else s["features"], k.before(U))
                if layer == 0:
                    act.dma_start(xin[0:r, k.u, :], x[bass.ds(k.t * P, r), :]).then_inc(s["loaded"][k.u], 16)
                else:
                    act.dma_start(sin[0:r, k.u, :], state[bass.ds(k.t * P, r), :]).then_inc(s["loaded"][k.u], 16)

            run_tiles(act, N, [(load, 6), (high, 3), (root if layer == 0 else parts, 5)])

        @block.tensor
        def _(pe):
            def transposes(k):
                transpose_tile(pe, s, g, k, psT[k.t_b], nrm[0:k.rows, k.t_b, :], "low")

            def multiply(k):
                r, b = k.rows, k.t_b
                pe.wait_ge(s["low"], k.ready())
                pe.wait_ge(s["xl"], k.before(2))
                multiply_split(pe, g, psL[b], b, 0, r).then_inc(s["lmul"], 1)
                pe.wait_ge(s["xr"], k.before(2))
                multiply_split(pe, g, psR[b], b, 1, r).then_inc(s["multiplied"], 1)

            run_tiles(pe, N, [(transposes, 3), (multiply, 2)])


def self_logit(dve, s, k, za, zb, zc, att, to):
    r, b = k.rows, k.t_b
    leaky(dve, s, k, za, zb)
    dve.wait_ge(s["lrelu"], k.ready())
    dve.wait_ge(s["logit"], k.before(2))
    dve.tensor_tensor(zc[0:r, b, :], zb[0:r, b, :], att[0:r, :], ALU.mult).then_inc(s["product"], 1)
    sum_heads(dve, s, k, zc, to)


def leaky(dve, s, k, za, zb):
    r, b = k.rows, k.t_b
    dve.wait_ge(s["product"], k.before(2))
    dve.scalar_tensor_tensor(zb[0:r, b, :], za[0:r, b, :], SLOPE, za[0:r, b, :],
                             ALU.mult, ALU.max).then_inc(s["lrelu"], 1)


def sum_heads(dve, s, k, zc, to):
    dve.wait_ge(s["product"], k.ready())
    dve.tensor_reduce(to, heads(zc[0:k.rows, k.t_b, :]), AX.X, ALU.add).then_inc(s["logit"], 1)


def edge_pass(nc, layer, g):
    N, E = g["N"], g["E"]
    att = g["vectors"][f"att{layer}"]
    xlG, xrG = g["xin"], g["xrS"]
    old = g["sin"]
    za, zb, zc, nrm = (g[k] for k in ("za", "zb", "zc", "nrm"))
    src_i, dst_i, dst_f = g["src_i"], g["dst_i"], g["dst_f"]
    banks, ident, ident16, earlier, head_rows = (g[k] for k in ("banks", "ident", "ident16", "earlier", "head_rows"))
    table, xr_table, state = g["xl_table"], g["xr_table"], g["state"]
    psF, psO, psB, psL = banks[0], banks[1], banks[2], banks[5]
    psD, psA = ([m[:, c0:c1] for m in banks[6:8]] for c0, c1 in ((0, P), (P, P + 1)))
    psS, psFs = banks[3][:, 0:H], banks[4][:, 0:2 * H]
    rows_gathered, got_state, put_state = g["rows_gathered"], g["state_gathered"], g["state_scattered"]
    rows_base = [layer * 32 * len(range(u, g["e_tiles"], U)) for u in range(U)]
    base = layer * 16 * g["e_tiles"]
    got_base = [layer * 16 * len(range(b, g["e_tiles"], 2)) for b in range(2)]

    def is_first(k):
        return type(k.i) is int and k.t == 0

    following = ("Wl1", "Wr1") if layer == 0 else ("gfc1T",)
    with ExitStack() as c:
        def sb(name, shape, dt=F32):
            return c.enter_context(nc.sbuf_tensor(f"{name}{layer}", shape, dt))

        w_loaded, w_high, w_low = own = [c.enter_context(nc.semaphore(f"{n}{layer}"))
                                         for n in ("next_w_loaded", "next_w_high", "next_w_low")]
        c.callback(lambda: clear(nc, own))
        s = phase_semaphores(nc, c, f"e{layer}", "apart index spread rowT eq duplicates scatter_float scatter z lrelu "
                             "product logit mask logitT rowsT everywhere peak shifted p weighted summed ordered "
                             "first passed passed_any absent fetch_float fetch written forwarded_small forwarded small selected "
                             "folded diffs factors rescaled sums_scaled snew onew")
        srcc = sb("srcc", [P, U, 1], I32)
        dstc = sb("dstc", [P, U, 1], I32)
        putc = sb("putc", [P, U, 1], I32)
        getc = sb("getc", [P, U, 1], I32)
        getf = sb("getf", [P, 2, 1])
        firsts = sb("firsts", [P, U, 1])
        passed = sb("passed", [P, U, P])
        absent = sb("absent", [P, U, 1])
        dstb = sb("dstb", [P, 2, P])
        eq = sb("eq", [P, U, P])
        mask = sb("mask", [P, U, P], BF16)
        tri = sb("tri", [P, 2, P])
        dup = sb("dup", [P, 2, 1])
        putf = sb("putf", [P, 2, 1])
        lg = sb("lg", [P, U, H])
        lgT = sb("lgT", [H, 2, P])
        pk = sb("pk", [P, U, H])
        prob = sb("prob", [P, U, H])
        df = sb("df", [P, 2, 2, H])
        new = sb("new", [P, 2, SW])
        s4 = sb("s4", [P, 2, H])
        block = c.enter_context(nc.Block())

        @block.sync
        def _(sp):
            load_weights(sp, g, following, w_loaded)

        @block.gpsimd
        def _(pool):
            lead(pool, s)

            def gather(k):
                r = k.rows
                pool.wait_ge(s["index"], k.ready())
                pool.wait_ge(s["weighted"], k.before(U))
                pool.wait_ge(s["z"], k.before(U))
                pool.sem_inc(s["apart"], 1)
                pool.indirect_dma_start(xlG[0:r, k.u, :], None, table[:, :],
                                        bass.IndirectOffsetOnAxis(srcc[0:r, k.u, :].bitcast(U32), 0)).then_inc(rows_gathered[k.u], 16)
                pool.indirect_dma_start(xrG[0:r, k.u, :], None, xr_table[:, :],
                                        bass.IndirectOffsetOnAxis(dstc[0:r, k.u, :].bitcast(U32), 0)).then_inc(rows_gathered[k.u], 16)

            def add(k):
                r, b = k.rows, k.t_b
                pool.wait_ge(rows_gathered[k.u], k.i * 32 + (32 + rows_base[k.u]))
                pool.wait_ge(s["lrelu"], k.before(2))
                pool.tensor_tensor(za[0:r, b, :], xlG[0:r, k.u, :], xrG[0:r, k.u, :], ALU.add).then_inc(s["z"], 1)

            def written(t):
                pool.wait_ge(put_state, t * 16 + (16 + base))
                pool.sem_inc(s["written"], 1)

            def fetch(k):
                r = k.rows
                if not (type(k.i) is int and k.t < 2):
                    pool.wait_ge(put_state, (k.t - 2) * 16 + (16 + base))
                pool.wait_ge(s["fetch"], k.ready())
                pool.wait_ge(s["selected"], k.before(U))
                pool.wait_ge(s["rescaled"], k.before(U))
                pool.sem_inc(s["apart"], 1)
                pool.indirect_dma_start(old[0:r, k.u, :], None, state[:, :],
                                        bass.IndirectOffsetOnAxis(getc[0:r, k.u, :].bitcast(U32), 0),
                                        bounds_check=N - 1, oob_is_err=False).then_inc(got_state[k.t_b], 16)

            def put(k):
                r = k.rows
                if not is_first(k):
                    written(k.t - 1)
                pool.wait_ge(s["scatter"], k.ready())
                pool.wait_ge(s["onew"], k.ready())
                pool.wait_ge(s["snew"], k.ready())
                pool.sem_inc(s["apart"], 1)
                pool.indirect_dma_start(state[:, :], bass.IndirectOffsetOnAxis(putc[0:r, k.u, :].bitcast(U32), 0),
                                        new[0:r, k.t_b, :], None, bounds_check=N - 1,
                                        oob_is_err=False).then_inc(put_state, 16)

            run_tiles(pool, E, [(put, 0), (gather, 6), (fetch, 2), (add, 5)], peel=1)
            written(g["e_tiles"] - 1)

        @block.vector
        def _(dve):
            def index(k):
                r = k.rows
                dve.wait_ge(s["z"], k.before(U))
                dve.tensor_copy(srcc[0:r, k.u, :], src_i[0:r, bass.ds(k.t, 1)])
                dve.tensor_copy(dstc[0:r, k.u, :], dst_i[0:r, bass.ds(k.t, 1)]).then_inc(s["index"], 1)

            def equal(k):
                r, b = k.rows, k.t_b
                dve.wait_ge(s["rowT"], k.ready())
                dve.wait_ge(s["summed"], k.before(U))
                dve.wait_ge(s["mask"], k.before(U))
                dve.tensor_scalar(eq[0:r, k.u, 0:r], psD[b][0:r, 0:r], dst_f[0:r, bass.ds(k.t, 1)], None,
                                  ALU.is_equal).then_inc(s["eq"], 1)

            def pass_on(k):
                r, b = k.rows, k.t_b
                dve.wait_ge(s["forwarded"], k.before(U))
                dve.wait_ge(s["first"], k.before(1))
                if is_first(k):
                    dve.memset(passed[:, k.u, :], 0.0).then_inc(s["passed"], 1)
                else:
                    dve.tensor_scalar(passed[:, k.u, 0:r], psD[b][:, 0:r], dst_f[:, bass.ds(k.t - 1, 1)],
                                      firsts[:, (k.u - 1) % U, :], ALU.is_equal, ALU.mult).then_inc(s["passed"], 1)

            def order(k):
                r, b = k.rows, k.t_b
                dve.wait_ge(s["eq"], k.ready())
                dve.wait_ge(s["duplicates"], k.before(2))
                dve.tensor_tensor(tri[0:r, b, 0:r], eq[0:r, k.u, 0:r], earlier[0:r, 0:r], ALU.mult).then_inc(s["ordered"], 1)

            def count(k):
                r, b = k.rows, k.t_b
                dve.wait_ge(s["ordered"], k.ready())
                dve.tensor_reduce(dup[0:r, b, :], tri[0:r, b, 0:r], AX.X, ALU.add).then_inc(s["duplicates"], 1)

            def destination(k):
                r, b = k.rows, k.t_b
                dve.wait_ge(s["duplicates"], k.ready())
                dve.tensor_scalar(putf[0:r, b, :], dup[0:r, b, :], SKIP, dst_f[0:r, bass.ds(k.t, 1)],
                                  ALU.mult, ALU.add).then_inc(s["scatter_float"], 1)
                dve.tensor_scalar(firsts[0:r, k.u, :], dup[0:r, b, :], 0.0, None, ALU.is_equal).then_inc(s["first"], 1)

            def destination_index(k):
                dve.wait_ge(s["scatter_float"], k.ready())
                dve.tensor_copy(putc[0:k.rows, k.u, :], putf[0:k.rows, k.t_b, :]).then_inc(s["scatter"], 1)

            def route(k):
                r, b = k.rows, k.t_b
                dve.wait_ge(s["passed_any"], k.ready())
                dve.tensor_scalar(getf[0:r, b, :], psA[b][0:r, :], SKIP, dst_f[0:r, bass.ds(k.t, 1)],
                                  ALU.mult, ALU.add).then_inc(s["fetch_float"], 1)
                dve.tensor_scalar(absent[0:r, k.u, :], psA[b][0:r, :], -1.0, 1.0, ALU.mult, ALU.add).then_inc(s["absent"], 1)

            def route_index(k):
                dve.wait_ge(s["fetch_float"], k.ready())
                dve.tensor_copy(getc[0:k.rows, k.u, :], getf[0:k.rows, k.t_b, :]).then_inc(s["fetch"], 1)

            def lrelu(k):
                dve.wait_ge(s["z"], k.ready())
                leaky(dve, s, k, za, zb)

            def product(k):
                r, b = k.rows, k.t_b
                dve.wait_ge(s["lrelu"], k.ready())
                dve.wait_ge(s["logit"], k.before(2))
                dve.tensor_tensor(zc[0:r, b, :], zb[0:r, b, :], att[0:r, :], ALU.mult).then_inc(s["product"], 1)

            def peak(k):
                r = k.rows
                dve.wait_ge(s["everywhere"], k.ready())
                dve.tensor_reduce(pk[0:r, k.u, :], heads(psB[0:r, :])[:, :, 0:r], AX.X, ALU.max).then_inc(s["peak"], 1)

            def shift(k):
                r = k.rows
                dve.wait_ge(s["peak"], k.ready())
                dve.tensor_tensor(prob[0:r, k.u, :], lg[0:r, k.u, :], pk[0:r, k.u, :], ALU.subtract).then_inc(s["shifted"], 1)

            def select_small(k):
                r, b = k.rows, k.t_b
                dve.wait_ge(got_state[b], k.i * (8 * U) + (16 * (k.u // 2) + 16 + got_base[b]))
                if not is_first(k):
                    dve.wait_ge(s["forwarded_small"], k.ready())
                    dve.scalar_tensor_tensor(old[0:r, k.u, D:SW], old[0:r, k.u, D:SW], absent[0:r, k.u, :],
                                             psFs[0:r, :], ALU.mult, ALU.add).then_inc(s["small"], 1)
                else:
                    dve.sem_inc(s["small"], 1)

            def maximum(k):
                r, b = k.rows, k.t_b
                dve.wait_ge(s["small"], k.ready())
                dve.tensor_tensor(new[0:r, b, D + H:SW], old[0:r, k.u, D + H:SW], pk[0:r, k.u, :], ALU.max).then_inc(s["folded"], 1)

            def differences(k):
                r, b = k.rows, k.t_b
                dve.wait_ge(s["folded"], k.ready())
                dve.tensor_tensor(df[0:r, b, 0, :], old[0:r, k.u, D + H:SW], new[0:r, b, D + H:SW], ALU.subtract)
                dve.tensor_tensor(df[0:r, b, 1, :], pk[0:r, k.u, :], new[0:r, b, D + H:SW], ALU.subtract).then_inc(s["diffs"], 1)

            def select(k):
                r = k.rows
                if not is_first(k):
                    dve.wait_ge(s["forwarded"], k.ready())
                    dve.scalar_tensor_tensor(old[0:r, k.u, 0:D], old[0:r, k.u, 0:D], absent[0:r, k.u, :],
                                             psF[0:r, :], ALU.mult, ALU.add).then_inc(s["selected"], 1)
                else:
                    dve.sem_inc(s["selected"], 1)

            def scale_sums(k):
                r, b = k.rows, k.t_b
                dve.wait_ge(s["factors"], k.ready())
                dve.wait_ge(s["summed"], k.ready())
                dve.tensor_tensor(s4[0:r, b, :], psS[0:r, :], df[0:r, b, 1, :], ALU.mult)
                dve.tensor_tensor(new[0:r, b, D:D + H], old[0:r, k.u, D:D + H], df[0:r, b, 0, :], ALU.mult).then_inc(s["sums_scaled"], 1)

            def add_sums(k):
                r, b = k.rows, k.t_b
                dve.wait_ge(s["sums_scaled"], k.ready())
                dve.tensor_tensor(new[0:r, b, D:D + H], new[0:r, b, D:D + H], s4[0:r, b, :], ALU.add).then_inc(s["snew"], 1)

            def accumulate(k):
                r, b = k.rows, k.t_b
                dve.wait_ge(s["rescaled"], k.ready())
                for h in range(H):
                    last = dve.scalar_tensor_tensor(new[0:r, b, h * C:(h + 1) * C], psO[0:r, h * C:(h + 1) * C],
                                                    df[0:r, b, 1, h:h + 1], new[0:r, b, h * C:(h + 1) * C],
                                                    ALU.mult, ALU.add)
                last.then_inc(s["onew"], 1)

            run_tiles(dve, E, [(equal, 4), (select_small, 0), (pass_on, 4), (maximum, 0), (order, 4),
                               (differences, 0), (select, 0), (count, 4), (destination, 4), (route, 3), (destination_index, 4),
                               (route_index, 3), (scale_sums, 0), (index, 7), (add_sums, 0),
                               (accumulate, 0), (lrelu, 4), (peak, 2), (product, 4), (shift, 2)], peel=1)
            split_low(dve, g, following, w_high, w_low)

        @block.scalar
        def _(act):
            def spread(k):
                r, b = k.rows, k.t_b
                act.wait_ge(s["rowT"], k.before(2))
                act.activation(dstb[0:r, b, :], dst_f[0:r, bass.ds(k.t, 1)].to_broadcast([r, P]), ACT.Copy).then_inc(s["spread"], 1)

            def hide(k):
                r = k.rows
                act.wait_ge(s["eq"], k.ready())
                act.wait_ge(s["everywhere"], k.before(U))
                act.activation(mask[0:r, k.u, 0:r], eq[0:r, k.u, 0:r], ACT.Copy, scale=BIG, bias=-BIG).then_inc(s["mask"], 1)

            def logit(k):
                r, b = k.rows, k.t_b
                act.wait_ge(s["product"], k.ready())
                act.wait_ge(s["logitT"], k.before(U))
                act.wait_ge(s["shifted"], k.before(U))
                for h in range(H):
                    z = zc[0:r, b, h * C:(h + 1) * C]
                    last = act.activation(z, z, ACT.Copy, accum_out=lg[0:r, k.u, h:h + 1])
                last.then_inc(s["logit"], 1)

            def transposed_logits(k):
                r, b = k.rows, k.t_b
                act.wait_ge(s["logitT"], k.ready())
                act.wait_ge(s["everywhere"], k.before(2))
                act.copy(lgT[:, b, 0:r], psL[0:H, 0:r]).then_inc(s["rowsT"], 1)

            def weigh(k):
                r, b = k.rows, k.t_b
                act.wait_ge(s["shifted"], k.ready())
                act.activation(prob[0:r, k.u, :], prob[0:r, k.u, :], ACT.Exp).then_inc(s["p"], 1)
                act.wait_ge(s["p"], k.ready())
                act.wait_ge(s["summed"], k.before(2))
                for h in range(H):
                    last = act.activation(nrm[0:r, b, h * C:(h + 1) * C], xlG[0:r, k.u, h * C:(h + 1) * C], ACT.Copy,
                                          scale=prob[0:r, k.u, h:h + 1])
                last.then_inc(s["weighted"], 1)

            def factors(k):
                r, b = k.rows, k.t_b
                act.wait_ge(s["diffs"], k.ready())
                act.activation(df[0:r, b, :, :], df[0:r, b, :, :], ACT.Exp).then_inc(s["factors"], 1)
                act.wait_ge(s["factors"], k.ready())
                act.wait_ge(s["selected"], k.ready())
                for h in range(H):
                    last = act.activation(new[0:r, b, h * C:(h + 1) * C], old[0:r, k.u, h * C:(h + 1) * C], ACT.Copy,
                                          scale=df[0:r, b, 0, h:h + 1])
                last.then_inc(s["rescaled"], 1)

            run_tiles(act, E, [(logit, 3), (factors, 0), (weigh, 1), (hide, 4), (transposed_logits, 3), (spread, 6)], peel=1)
            split_high(act, g, following, w_loaded, w_high)

        @block.tensor
        def _(pe):
            def rows(k):
                r, b = k.rows, k.t_b
                pe.wait_ge(s["spread"], k.ready())
                pe.wait_ge(s["eq"], k.before(2))
                pe.wait_ge(s["passed"], k.before(2))
                pe.wait_ge(s["fetch_float"], k.before(2))
                pe.wait_ge(s["absent"], k.before(2))
                pe.transpose(psD[b][:, 0:r], dstb[0:r, b, :], ident[0:r, 0:r]).then_inc(s["rowT"], 1)

            def logits_across(k):
                r, b = k.rows, k.t_b
                pe.wait_ge(s["logit"], k.ready())
                pe.wait_ge(s["rowsT"], k.before(1))
                pe.transpose(psL[0:H, 0:r], lg[0:r, k.u, :], ident[0:r, 0:r]).then_inc(s["logitT"], 1)

            def everywhere(k):
                r, b = k.rows, k.t_b
                pe.wait_ge(s["rowsT"], k.ready())
                pe.wait_ge(s["mask"], k.ready())
                pe.wait_ge(s["peak"], k.before(1))
                pe.matmul(heads(psB[0:r, :])[:, :, 0:r], ident16[0:r, 0:r],
                          mask[0:r, k.u, 0:r].unsqueeze(1).to_broadcast([r, H, r]), start=True, stop=False)
                for h in range(H):
                    last = pe.matmul(psB[0:r, h * P:h * P + r], head_rows[:, h, 0:r], lgT[:, b, 0:r],
                                     start=False, stop=(h == H - 1))
                last.then_inc(s["everywhere"], 1)

            def nodes_passed(k):
                r, b = k.rows, k.t_b
                pe.wait_ge(s["passed"], k.ready())
                pe.matmul(psA[b][0:r, :], passed[:, k.u, 0:r], g["ones"][:, 0:1], start=True, stop=True).then_inc(s["passed_any"], 1)

            def forward(k):
                r, b = k.rows, k.t_b
                if is_first(k):
                    pe.sem_inc(s["forwarded_small"], 1)
                    pe.sem_inc(s["forwarded"], 1)
                    return
                pe.wait_ge(s["snew"], k.before(1))
                pe.matmul(psFs[0:r, :], passed[:, k.u, 0:r], new[:, 1 - b, D:SW], start=True, stop=True).then_inc(s["forwarded_small"], 1)
                pe.wait_ge(s["onew"], k.before(1))
                pe.matmul(psF[0:r, :], passed[:, k.u, 0:r], new[:, 1 - b, 0:D], start=True, stop=True).then_inc(s["forwarded"], 1)

            def sums(k):
                r, b = k.rows, k.t_b
                pe.wait_ge(s["weighted"], k.ready())
                pe.wait_ge(s["onew"], k.before(1))
                pe.matmul(psO[0:r, :], eq[0:r, k.u, 0:r], nrm[0:r, b, :], start=True, stop=True)
                pe.matmul(psS[0:r, :], eq[0:r, k.u, 0:r], prob[0:r, k.u, :], start=True, stop=True).then_inc(s["summed"], 1)

            run_tiles(pe, E, [(nodes_passed, 4), (rows, 5), (logits_across, 3), (forward, 1), (sums, 1), (everywhere, 3)], peel=1)


def gate(nc, x, g, inputs):
    N = g["N"]
    bias = g["vectors"]["bias1"]
    xin, sin, nrm, x1 = g["xin"], g["sin"], g["nrm"], g["xrS"]
    za, scr, st6, mv, rs4, moments, unit_sum = (g[k] for k in ("za", "scr", "st6", "mv", "rs4", "moments", "unit_sum"))
    banks, state, x1_table = g["banks"], g["state"], g["x1_table"]
    psT, psG = banks[0:2], banks[2:4]
    with ExitStack() as c:
        s = phase_semaphores(nc, c, "g", "apart saved stats aggregated scale inverted shift kept inverse biased x1 normed "
                             "transposed high low multiplied units added", ("loaded", "stored"))
        block = c.enter_context(nc.Block())

        @block.gpsimd
        def _(pool):
            lead(pool, s)

            def add_bias(k):
                r, b = k.rows, k.t_b
                pool.wait_ge(s["loaded"][k.u], k.i * 32 + 32)
                pool.wait_ge(s["x1"], k.before(2))
                pool.tensor_tensor(scr[0:r, b, :], xin[0:r, k.u, :], bias[0:r, :], ALU.add).then_inc(s["biased"], 1)

            def accumulate(k):
                r, b = k.rows, k.t_b
                pool.wait_ge(s["units"], k.ready())
                pool.wait_ge(s["added"], k.before(1))
                pool.tensor_tensor(unit_sum[0:r, :], unit_sum[0:r, :], za[0:r, b, :], ALU.add).then_inc(s["added"], 1)

            run_tiles(pool, N, [(add_bias, 6), (accumulate, 0)])

        @block.sync
        def _(sp):
            inputs["load"](sp)

            def store(k):
                r = k.rows
                sp.wait_ge(s["x1"], k.ready())
                sp.dma_start(x1_table[bass.ds(k.t * P, r), :], x1[0:r, k.u, :]).then_inc(s["stored"][k.u], 16)

            def confirm(k):
                sp.wait_ge(s["stored"][k.u], k.i * 16 + 16)
                sp.sem_inc(s["saved"], 1)

            run_tiles(sp, N, [(store, 1), (confirm, 0)])
            for u in range(U):
                sp.wait_ge(s["stored"][u], 16 * len(range(u, g["n_tiles"], U)))

        @block.vector
        def _(dve):
            def inverse(k):
                r, b = k.rows, k.t_b
                dve.wait_ge(s["loaded"][k.u], k.i * 32 + 32)
                dve.wait_ge(s["x1"], k.before(2))
                dve.reciprocal(rs4[0:r, b, :], sin[0:r, k.u, D:D + H]).then_inc(s["inverse"], 1)

            def residual(k):
                r, b = k.rows, k.t_b
                dve.wait_ge(s["inverse"], k.ready())
                dve.wait_ge(s["biased"], k.ready())
                dve.wait_ge(s["saved"], k.before(U))
                for h in range(H):
                    last = dve.scalar_tensor_tensor(x1[0:r, k.u, h * C:(h + 1) * C], sin[0:r, k.u, h * C:(h + 1) * C],
                                                    rs4[0:r, b, h:h + 1], scr[0:r, b, h * C:(h + 1) * C],
                                                    ALU.mult, ALU.add)
                last.then_inc(s["x1"], 1)

            def measure(k):
                dve.wait_ge(s["x1"], k.ready())
                dve.wait_ge(s["normed"], k.before(2))
                dve.wait_ge(s["kept"], k.before(2))
                moments_of(dve, s, k, x1[0:k.rows, k.u, :], st6[0:k.rows, k.t_b, :], mv[0:k.rows, k.t_b, :])

            def invert(k):
                negative_mean(dve, s, k, mv[0:k.rows, k.t_b, :])

            def keep(k):
                r, b = k.rows, k.t_b
                dve.wait_ge(s["shift"], k.ready())
                dve.tensor_copy(moments[0:r, bass.ds(k.t, 1), :].rearrange("p a b -> p (a b)"),
                                mv[0:r, b, :]).then_inc(s["kept"], 1)

            def low(k):
                dve.wait_ge(s["multiplied"], k.before(2))
                take_low(dve, s, g, k, psT[k.t_b])

            run_tiles(dve, N, [(invert, 3), (measure, 4), (low, 2), (residual, 5), (keep, 3), (inverse, 6)])

        @block.scalar
        def _(act):
            def root(k):
                deviation(act, s, k, mv[0:k.rows, k.t_b, :], g["eps"])

            def norm(k):
                r, b = k.rows, k.t_b
                act.wait_ge(s["shift"], k.ready())
                act.wait_ge(s["transposed"], k.before(2))
                act.activation(nrm[0:r, b, :], x1[0:r, k.u, :], ACT.Identity, scale=mv[0:r, b, 1:2],
                               bias=mv[0:r, b, 0:1]).then_inc(s["normed"], 1)

            def high(k):
                copy_high(act, s, g, k, psT[k.t_b])

            def units(k):
                r, b = k.rows, k.t_b
                act.wait_ge(s["multiplied"], k.ready())
                act.wait_ge(s["added"], k.before(2))
                act.activation(za[0:r, b, :], psG[b][0:r, :], ACT.Relu).then_inc(s["units"], 1)

            def load(k):
                r = k.rows
                act.wait_ge(s["x1"], k.before(U))
                act.wait_ge(s["biased"], k.before(U))
                act.dma_start(sin[0:r, k.u, :], state[bass.ds(k.t * P, r), :]).then_inc(s["loaded"][k.u], 16)
                act.dma_start(xin[0:r, k.u, :], x[bass.ds(k.t * P, r), :]).then_inc(s["loaded"][k.u], 16)

            run_tiles(act, N, [(load, 7), (high, 2), (norm, 3), (units, 0), (root, 4)])

        @block.tensor
        def _(pe):
            def transposes(k):
                transpose_tile(pe, s, g, k, psT[k.t_b], nrm[0:k.rows, k.t_b, :], "low")

            def multiply(k):
                r, b = k.rows, k.t_b
                pe.wait_ge(s["low"], k.ready())
                pe.wait_ge(s["units"], k.before(2))
                multiply_split(pe, g, psG[b], b, 0, r, more=True)
                pe.matmul(psG[b][0:r, :], g["bias_ones"][:, 0:r], g["unit_bias"][:, :],
                          start=False, stop=True).then_inc(s["multiplied"], 1)

            run_tiles(pe, N, [(transposes, 2), (multiply, 1)])


def merge_inputs(nc, c, w, g):
    w1m, b1m = g["w1m"], g["b1m"]

    def sb(name, shape):
        return c.enter_context(nc.sbuf_tensor(name, shape, F32))

    tv1 = sb("tv1", [P, KC, NE, F])
    w2m = sb("w2m", [FS, D])
    tv2 = sb("tv2", [FS, NE, D])
    tvb1 = sb("tvb1", [3 * F, NE])
    gfc2T = sb("gfc2T_sb", [P, KC, NE])
    gfc2b = sb("gfc2b_sb", [P, NE])
    norm_rows = {k: sb(k + "_rows", [NE + 1, D]) for k in ("ln_g", "ln_b")}
    loaded = c.enter_context(nc.semaphore("merge_loaded"))
    c.callback(lambda: clear(nc, [loaded]))
    loads = KC + 3 + 4 * 3 + 2 * 2 + 2 * 2

    def load(sp):
        for cc in range(KC):
            sp.dma_start(tv1[:, cc, :, :], w["tv_W1T"][cc * P:(cc + 1) * P, :, :]).then_inc(loaded, 16)
        sp.dma_start(w1m[:, :, 0, :], w["W1T"].rearrange("(c p) f -> p c f", p=P)).then_inc(loaded, 16)
        for q in range(0, 3 * F, F):
            sp.dma_start(tv2[q:q + F, :, :], w["tv_W2T"]).then_inc(loaded, 16)
            sp.dma_start(w2m[q:q + F, :], w["W2T"]).then_inc(loaded, 16)
            sp.dma_start(tvb1[q:q + F, :], w["tv_b1T"]).then_inc(loaded, 16)
            sp.dma_start(b1m[q:q + F, :], w["b1"].rearrange("(f a) -> f a", a=1)).then_inc(loaded, 16)
        for q in (3 * F, 3 * F + 1):
            sp.dma_start(tv2[q:q + 1, :, :], w["tv_b2"].rearrange("(a e) d -> a e d", a=1)).then_inc(loaded, 16)
            sp.dma_start(w2m[q:q + 1, :], w["b2"].rearrange("(a d) -> a d", a=1)).then_inc(loaded, 16)
        sp.dma_start(gfc2T[:, :, :], w["gfc2T"].rearrange("(c p) e -> p c e", p=P)).then_inc(loaded, 16)
        sp.dma_start(gfc2b[:, :], bcast(w["gfc2_b"])).then_inc(loaded, 16)
        for k, rows in norm_rows.items():
            sp.dma_start(rows[0:1, :], w[k].rearrange("(a d) -> a d", a=1)).then_inc(loaded, 16)
            sp.dma_start(rows[1:NE + 1, :], w["tv_" + k]).then_inc(loaded, 16)

    return dict(tv1=tv1, w2m=w2m, tv2=tv2, tvb1=tvb1, gfc2T=gfc2T, gfc2b=gfc2b, norm_rows=norm_rows, load=load,
                loaded=loaded, all_loaded=16 * loads)


def merge(nc, g, inputs):
    N = g["N"]
    banks, ones, unit_sum = g["banks"], g["ones"], g["unit_sum"]
    tv1, w2m, tv2, tvb1, gfc2T, gfc2b, norm_rows, loaded, all_loaded = (inputs[k] for k in (
        "tv1", "w2m", "tv2", "tvb1", "gfc2T", "gfc2b", "norm_rows", "loaded", "all_loaded"))
    w1m, w2parts, b1m = g["w1m"], g["w2parts"], g["b1m"]
    with ExitStack() as c:
        def sb(name, shape):
            return c.enter_context(nc.sbuf_tensor(name, shape, F32))

        high = c.enter_context(nc.sbuf_tensor("w2_high", [FS, D], F32R))
        is_low = sb("is_low", [FS, 1])
        norm_weights = sb("norm_weights", [NE + 1, P])
        mean = sb("mean", [P, KC])
        spread = sb("mean_spread", [P, KC, P])
        gv = sb("gv", [P, NE])
        weights_set = c.enter_context(nc.semaphore("norm_weights_set"))
        norm_merged = c.enter_context(nc.semaphore("norm_merged"))
        summed = c.enter_context(nc.semaphore("units_summed"))
        spread_s = c.enter_context(nc.semaphore("mean_spread"))
        gated = c.enter_context(nc.semaphore("gate_product"))
        chain = c.enter_context(nc.semaphore("merge_chain"))
        c.callback(lambda: clear(nc, [weights_set, norm_merged, summed, spread_s, gated, chain]))
        block = c.enter_context(nc.Block())

        @block.sync
        def _(sp):
            sp.wait_ge(loaded, all_loaded)

        @block.tensor
        def _(pe):
            for cc in range(KC):
                last = pe.matmul(banks[0][:, cc:cc + 1], unit_sum[:, cc * P:(cc + 1) * P], ones[:, 0:1],
                                 start=True, stop=True)
            last.then_inc(summed, 1)
            pe.wait_ge(weights_set, 2)
            pe.wait_ge(loaded, all_loaded)
            for n, rows in enumerate(norm_rows.values()):
                last = pe.matmul(banks[2 + n][:, :], norm_weights[:, :], rows[:, :], start=True, stop=True)
            last.then_inc(norm_merged, 1)
            pe.wait_ge(spread_s, 1)
            for cc in range(KC):
                last = pe.matmul(banks[1][:, 0:NE], spread[:, cc, :], gfc2T[:, cc, :],
                                 start=(cc == 0), stop=(cc == KC - 1))
            last.then_inc(gated, 1)

        @block.vector
        def _(dve):
            n = 0

            def link(ins):
                nonlocal n
                n += 1
                ins.then_inc(chain, 1)
                dve.wait_ge(chain, n)

            dve.memset(norm_weights[:, :], MERGE).then_inc(weights_set, 1)
            dve.wait_ge(weights_set, 1)
            dve.memset(norm_weights[0:1, :], 1.0 - NE * MERGE).then_inc(weights_set, 1)
            link(dve.memset(is_low[:, :], 0.0))
            link(dve.memset(is_low[2 * F:FS, :], -1.0))
            link(dve.memset(is_low[3 * F:3 * F + 1, :], 0.0))
            dve.wait_ge(summed, 1)
            link(dve.tensor_scalar(mean[:, :], banks[0][:, 0:KC], 1.0 / N, None, ALU.mult))
            dve.tensor_copy(spread[:, :, :], mean[:, :].unsqueeze(2).to_broadcast([P, KC, P])).then_inc(spread_s, 1)
            dve.wait_ge(gated, 1)
            link(dve.tensor_tensor(gv[:, :], banks[1][:, 0:NE], gfc2b[:, :], ALU.add))
            dve.wait_ge(loaded, all_loaded)
            for e in range(NE):
                for to, tv, r in ((w1m[:, :, 0, :], tv1[:, :, e, :], P), (w2m[:, :], tv2[:, e, :], FS),
                                  (b1m[:, :], tvb1[:, e:e + 1], 3 * F)):
                    link(dve.scalar_tensor_tensor(to, tv, gv[0:r, e:e + 1], to, ALU.mult, ALU.add))
            for q in (1, 2):
                dve.tensor_copy(w1m[:, :, q, :], w1m[:, :, 0, :])
            link(dve.tensor_copy(high[:, :], w2m[:, :]))
            link(dve.scalar_tensor_tensor(w2parts[:, :], high[:, :].bitcast(F32), is_low[:, :], w2m[:, :],
                                          ALU.mult, ALU.add))
            dve.wait_ge(norm_merged, 1)
            dve.tensor_copy(g["ln_g"][:, :], banks[2][:, :])
            dve.tensor_copy(g["ln_b"][:, :], banks[3][:, :])


def ffn(nc, out, g):
    N = g["N"]
    x1, nrm, nrmT = g["xin"], g["xrS"], g["scr"]
    shifted, outS, st6, moments, mv = (g[k] for k in ("sin", "xlS", "st6", "moments", "mv"))
    lng, lnb = g["ln_g"], g["ln_b"]
    w1m, w2parts, b1m, hidden = g["w1m"], g["w2parts"], g["b1m"], g["hidden"]
    banks, ident, x1_table = g["banks"], g["ident"], g["x1_table"]
    psT, psH, psO = banks[0:2], banks[2:4], banks[4:6]
    with ExitStack() as c:
        s = phase_semaphores(nc, c, "f", "apart saved normed transposed featT first units full hidden second result stats aggregated scale inverted shift "
                   "centred shifted scaled final", ("loaded", "stored"))
        full = c.enter_context(nc.sbuf_tensor("units_full", [2 * F, 2, P], F32))
        block = c.enter_context(nc.Block())

        @block.gpsimd
        def _(pool):
            lead(pool, s)

            def add_offset(k):
                r = k.rows
                pool.wait_ge(s["loaded"][k.u], k.i * 16 + 16)
                pool.wait_ge(s["final"], k.before(U))
                pool.tensor_tensor(shifted[0:r, k.u, 0:D], x1[0:r, k.u, :], lnb[0:r, :], ALU.add).then_inc(s["shifted"], 1)

            def scale(k):
                y = outS[0:k.rows, k.u, 0:D]
                pool.wait_ge(s["centred"], k.ready())
                pool.tensor_tensor(y, y, lng[0:k.rows, :], ALU.mult).then_inc(s["scaled"], 1)

            run_tiles(pool, N, [(scale, 1), (add_offset, 5)])

        @block.sync
        def _(sp):
            def store(k):
                r = k.rows
                sp.wait_ge(s["final"], k.ready())
                sp.dma_start(out[bass.ds(k.t * P, r), :], outS[0:r, k.u, 0:D]).then_inc(s["stored"][k.u], 16)

            def confirm(k):
                sp.wait_ge(s["stored"][k.u], k.i * 16 + 16)
                sp.sem_inc(s["saved"], 1)

            run_tiles(sp, N, [(store, 1), (confirm, 0)])
            for u in range(U):
                sp.wait_ge(s["stored"][u], 16 * len(range(u, g["n_tiles"], U)))

        @block.vector
        def _(dve):
            def invert(k):
                negative_mean(dve, s, k, mv[0:k.rows, k.t_b, :])

            def low_units(k):
                b, r = k.t_b, k.rows
                low = slice(F, 2 * F)
                dve.wait_ge(s["units"], k.ready())
                dve.wait_ge(s["hidden"], k.before(2))
                dve.tensor_scalar(full[low, b, 0:r], psH[b][low, 0:r], b1m[low, 0:1], 0.0, ALU.add, ALU.max).then_inc(s["full"], 1)
                dve.wait_ge(s["full"], k.ready())
                dve.tensor_tensor(hidden[low, b, 0:r], full[low, b, 0:r], hidden[low, b, 0:r].bitcast(F32),
                                  ALU.subtract).then_inc(s["hidden"], 1)

            def result(k):
                r, b = k.rows, k.t_b
                dve.wait_ge(s["second"], k.ready())
                dve.wait_ge(s["saved"], k.before(U))
                dve.tensor_tensor(outS[0:r, k.u, 0:D], psO[b][0:r, :], nrm[0:r, k.u, :], ALU.add).then_inc(s["result"], 1)

            def measure(k):
                r, b = k.rows, k.t_b
                dve.wait_ge(s["result"], k.ready())
                dve.wait_ge(s["centred"], k.before(2))
                moments_of(dve, s, k, outS[0:r, k.u, 0:D], st6[0:r, b, :], mv[0:r, b, :])

            def final(k):
                r = k.rows
                y = outS[0:r, k.u, 0:D]
                dve.wait_ge(s["scaled"], k.ready())
                dve.wait_ge(s["shifted"], k.ready())
                dve.tensor_tensor(y, y, shifted[0:r, k.u, 0:D], ALU.add).then_inc(s["final"], 1)

            run_tiles(dve, N, [(invert, 1), (measure, 2), (final, 0), (low_units, 4), (result, 3)])

        @block.scalar
        def _(act):
            def norm(k):
                r = k.rows
                act.wait_ge(s["loaded"][k.u], k.i * 16 + 16)
                act.wait_ge(s["result"], k.before(U))
                m = moments[0:r, bass.ds(k.t, 1), :].rearrange("p a b -> p (a b)")
                act.activation(nrm[0:r, k.u, :], x1[0:r, k.u, :], ACT.Identity, scale=m[:, 1:2],
                               bias=m[:, 0:1]).then_inc(s["normed"], 1)

            def copy_transposed(k):
                r, b = k.rows, k.t_b
                act.wait_ge(s["transposed"], k.ready())
                act.wait_ge(s["first"], k.before(2))
                act.copy(nrmT[:, b, :].rearrange("p (c n) -> p c n", c=KC)[:, :, 0:r],
                         psT[b][:, :].rearrange("p (c n) -> p c n", c=KC)[:, :, 0:r]).then_inc(s["featT"], 1)

            def units(k):
                r, b = k.rows, k.t_b
                act.wait_ge(s["first"], k.ready())
                act.wait_ge(s["second"], k.before(2))
                act.activation(hidden[0:3 * F, b, 0:r], psH[b][0:3 * F, 0:r], ACT.Relu, bias=b1m[:, 0:1]).then_inc(s["units"], 1)

            def spread(k):
                deviation(act, s, k, mv[0:k.rows, k.t_b, :], g["eps"])

            def centre(k):
                r, b = k.rows, k.t_b
                y = outS[0:r, k.u, 0:D]
                act.wait_ge(s["shift"], k.ready())
                act.activation(y, y, ACT.Identity, scale=mv[0:r, b, 1:2], bias=mv[0:r, b, 0:1]).then_inc(s["centred"], 1)

            def load(k):
                r = k.rows
                act.wait_ge(s["shifted"], k.before(U))
                act.wait_ge(s["normed"], k.before(U))
                act.dma_start(x1[0:r, k.u, :], x1_table[bass.ds(k.t * P, r), :]).then_inc(s["loaded"][k.u], 16)

            run_tiles(act, N, [(load, 7), (norm, 6), (units, 4), (copy_transposed, 5), (centre, 1), (spread, 2)])

        @block.tensor
        def _(pe):
            def transposes(k):
                r, b = k.rows, k.t_b
                pe.wait_ge(s["normed"], k.ready())
                pe.wait_ge(s["featT"], k.before(2))
                for c in range(KC):
                    last = pe.transpose(psT[b][:, c * P:c * P + r], nrm[0:r, k.u, c * P:(c + 1) * P], ident[0:r, 0:r])
                last.then_inc(s["transposed"], 1)

            def first(k):
                r, b = k.rows, k.t_b
                pe.wait_ge(s["featT"], k.ready())
                pe.wait_ge(s["hidden"], k.before(2))
                for c in range(KC):
                    last = pe.matmul(psH[b][0:3 * F, 0:r], w1m[:, c, :, :].rearrange("p a f -> p (a f)"), nrmT[:, b, c * P:c * P + r],
                                     start=(c == 0), stop=(c == KC - 1))
                last.then_inc(s["first"], 1)

            def second(k):
                r, b = k.rows, k.t_b
                pe.wait_ge(s["hidden"], k.ready())
                pe.wait_ge(s["result"], k.before(2))
                pe.matmul(psO[b][0:r, :], hidden[:, b, 0:r], w2parts[:, :], start=True, stop=True).then_inc(s["second"], 1)

            run_tiles(pe, N, [(second, 3), (first, 5), (transposes, 6)])


def kernel(**a):
    import concourse.bacc as bacc
    from concourse.bass_utils import run_bass_kernel_spmd

    nc = bacc.Bacc("TRN2", target_bir_lowering=False, num_devices=1)
    flat = {
        "x": a["x"], "src": a["src"], "dst": a["dst"],
        "gfc1T": np.asarray(a["L0_ffn_gfc1_w"]).T, "gfc1_b": a["L0_ffn_gfc1_b"],
        "gfc2T": np.asarray(a["L0_ffn_gfc2_w"]).T, "gfc2_b": a["L0_ffn_gfc2_b"],
        "W1T": np.asarray(a["L0_ffn_W1"]).T, "b1": a["L0_ffn_b1"],
        "W2T": np.asarray(a["L0_ffn_W2"]).T, "b2": a["L0_ffn_b2"],
        "ln_g": a["L0_ffn_ln_g"], "ln_b": a["L0_ffn_ln_b"],
        "tv_W1T": np.asarray(a["L0_ffn_tv_W1"]).transpose(2, 0, 1),
        "tv_b1T": np.asarray(a["L0_ffn_tv_b1"]).T,
        "tv_W2T": np.asarray(a["L0_ffn_tv_W2"]).transpose(2, 0, 1),
        "tv_b2": a["L0_ffn_tv_b2"], "tv_ln_g": a["L0_ffn_tv_ln_g"], "tv_ln_b": a["L0_ffn_tv_ln_b"],
    }
    for v in ("Wl", "bl", "Wr", "br", "bias"):
        for n in range(2):
            flat[f"{v}{n}"] = a[f"L0_gnn_{v}{n}"]
    for n in range(2):
        flat[f"att{n}"] = np.asarray(a[f"L0_gnn_att{n}"]).reshape(-1)
    arrays, w = {}, {}
    for name, v in flat.items():
        v = np.ascontiguousarray(v)
        arrays[f"in_{name}"] = v
        w[name] = nc.dram_tensor(f"in_{name}", v.shape, mybir.dt.from_np(v.dtype), kind="ExternalInput").ap()
    shape = np.asarray(a["x"]).shape
    out = nc.dram_tensor("out", shape, F32, kind="ExternalOutput").ap()
    build(nc, w["x"], w["src"], w["dst"], w, out)
    r = run_bass_kernel_spmd(nc, [arrays], core_ids=[0])
    return r.results[0]["out"]
```
